# Optimizing a Trainium2 kernel written in Bass

```python
import numpy as np
import jax
import jax.numpy as jnp

def _softmax(x, axis=-1):
    return jax.nn.softmax(x, axis=axis)

def _gelu(x):
    return jax.nn.gelu(x, approximate=True)

def _silu(x):
    return jax.nn.silu(x)

def _sigmoid(x):
    return jax.nn.sigmoid(x)

def _layernorm(x, axis=-1, eps=1e-05):
    m = jnp.mean(x, axis=axis, keepdims=True)
    v = jnp.var(x, axis=axis, keepdims=True)
    return (x - m) / jnp.sqrt(v + eps)

def _scatter_add(tgt, idx, src, axis=0):
    return tgt.at[idx].add(src)

def _segment_sum(src, seg, n):
    return jax.ops.segment_sum(src, seg, n)
kernel_name = 'mk_seq_postln_d1_jaxref_r8_70a1f8'

def setup_inputs(seed: int=0):
    np.random.seed(seed)
    _w = jnp.asarray

    def _L0_attn_setup():
        import jax, jax.numpy as jnp
        import numpy as np
        LN_EPS = 1e-05
        key = jax.random.key(seed)
        ks = jax.random.split(key, 5)
        B, S, E, H = (4, 128, 128, 16)
        sd = E ** (-0.5)
        return {'x': jax.random.normal(ks[0], (B, S, E), jnp.float32), 'Wq': jax.random.normal(ks[1], (E, E), jnp.float32) * sd, 'Wk': jax.random.normal(ks[2], (E, E), jnp.float32) * sd, 'Wv': jax.random.normal(ks[3], (E, E), jnp.float32) * sd, 'bias_table': jax.random.normal(ks[4], (2 * S - 1, H), jnp.float32) * 0.02, 'ln_gamma': jnp.ones((E,), jnp.float32), 'ln_beta': jnp.zeros((E,), jnp.float32)}
    _L0_attn_in = _L0_attn_setup()

    def _L0_ffn_setup():
        import jax, jax.numpy as jnp
        import numpy as np
        B, T, D, FF, E, TOP_K = (8, 256, 128, 512, 8, 2)
        key = jax.random.key(seed)
        kx, kr, k1, k2 = jax.random.split(key, 4)
        x = jax.random.normal(kx, (B, T, D), dtype=jnp.float32)
        Wr = jax.random.normal(kr, (E, D), dtype=jnp.float32) * 0.02
        W1 = jax.random.normal(k1, (E, D, FF), dtype=jnp.float32) * 0.02
        W2 = jax.random.normal(k2, (E, FF, D), dtype=jnp.float32) * 0.02
        return {'x': x, 'Wr': Wr, 'W1': W1, 'W2': W2}
    _L0_ffn_in = _L0_ffn_setup()
    _d = {'L0_attn_x': _L0_attn_in['x'], 'L0_attn_Wq': _L0_attn_in['Wq'], 'L0_attn_Wk': _L0_attn_in['Wk'], 'L0_attn_Wv': _L0_attn_in['Wv'], 'L0_attn_bias_table': _L0_attn_in['bias_table'], 'L0_attn_ln_gamma': _L0_attn_in['ln_gamma'], 'L0_attn_ln_beta': _L0_attn_in['ln_beta'], 'L0_ffn_Wr': _L0_ffn_in['Wr'], 'L0_ffn_W1': _L0_ffn_in['W1'], 'L0_ffn_W2': _L0_ffn_in['W2']}
    _x0 = _d['L0_attn_x']
    _d['L0_attn_x'] = jax.random.normal(jax.random.fold_in(jax.random.key(seed), 1), (2, 1024, 128), dtype=_x0.dtype)
    del _x0
    return _d

def reference(L0_attn_x, L0_attn_Wq, L0_attn_Wk, L0_attn_Wv, L0_attn_bias_table, L0_attn_ln_gamma, L0_attn_ln_beta, L0_ffn_Wr, L0_ffn_W1, L0_ffn_W2):

    def _L0_attn_ref(x, Wq, Wk, Wv, bias_table, ln_gamma, ln_beta):
        import jax, jax.numpy as jnp
        import numpy as np
        LN_EPS = 1e-05
        B, S, E = x.shape
        H = bias_table.shape[1]
        d = E // H
        scale = E ** (-0.5)
        q = (x @ Wq.T).reshape(B, S, H, d).transpose(0, 2, 1, 3)
        k = (x @ Wk.T).reshape(B, S, H, d).transpose(0, 2, 1, 3)
        v = (x @ Wv.T).reshape(B, S, H, d).transpose(0, 2, 1, 3)
        attn = jax.nn.softmax(jnp.einsum('bhsd,bhtd->bhst', q, k) * scale, axis=-1)
        rel_idx = jnp.arange(S)[:, None] - jnp.arange(S)[None, :] + (S - 1)
        rel_bias = bias_table[rel_idx].transpose(2, 0, 1)
        attn = attn + rel_bias[None]
        out = jnp.einsum('bhst,bhtd->bhsd', attn, v)
        out = out.transpose(0, 2, 1, 3).reshape(B, S, E)
        mu = out.mean(-1, keepdims=True)
        var = out.var(-1, keepdims=True)
        out = (out - mu) * jax.lax.rsqrt(var + LN_EPS) * ln_gamma + ln_beta
        return out

    def _L0_ffn_ref(x, Wr, W1, W2):
        import jax, jax.numpy as jnp
        import numpy as np
        B, T, D, FF, E, TOP_K = (8, 256, 128, 512, 8, 2)
        Bs, Ts, Ds = x.shape
        Ne = Wr.shape[0]
        xf = x.reshape(-1, Ds)
        N = xf.shape[0]
        logits = xf @ Wr.T
        topk_vals, topk_idx = jax.lax.top_k(logits, TOP_K)
        w = jax.nn.softmax(topk_vals.astype(jnp.float32), axis=-1).astype(x.dtype)
        idx_flat = topk_idx.reshape(-1)
        w_flat = w.reshape(-1)
        sort_idx = jnp.argsort(idx_flat)
        rev = sort_idx // TOP_K
        sw = w_flat[sort_idx]
        perm = xf[rev]
        S = perm.shape[0]
        chunks = perm.reshape(Ne, S // Ne, Ds)
        h = jax.nn.gelu(jnp.einsum('ecd,edf->ecf', chunks, W1), approximate=False)
        eo = jnp.einsum('ecf,efd->ecd', h, W2).reshape(S, Ds)
        out = jnp.zeros((N, Ds), dtype=x.dtype).at[rev].add(eo * sw[:, None])
        return out.reshape(Bs, Ts, Ds)
    x = L0_attn_x
    x = _layernorm(x + _L0_attn_ref(x, L0_attn_Wq, L0_attn_Wk, L0_attn_Wv, L0_attn_bias_table, L0_attn_ln_gamma, L0_attn_ln_beta), axis=-1)
    x = _layernorm(x + _L0_ffn_ref(x, L0_ffn_Wr, L0_ffn_W1, L0_ffn_W2), axis=-1)
    return x

_drawn_inputs = setup_inputs


def setup_inputs(seed=0):
    import zlib

    import numpy as np

    out = dict(_drawn_inputs(seed))
    spreads = {'L0_attn_ln_gamma': (1.0, 0.2), 'L0_attn_ln_beta': (0.0, 0.1)}
    factors = {}
    for name, (base, spread) in spreads.items():
        noise = np.random.default_rng([zlib.crc32(name.encode()), seed]).standard_normal(out[name].shape)
        drawn = base * np.exp(spread * noise) if base else spread * noise
        out[name] = jnp.asarray(drawn.astype(out[name].dtype))
    for name, factor in factors.items():
        out[name] = (out[name] * factor).astype(out[name].dtype)
    return out
```

```python
from contextlib import ExitStack

import numpy as np

import concourse.bass as bass
from concourse import mybir

F32 = mybir.dt.float32
BF16 = mybir.dt.bfloat16
I32 = mybir.dt.int32
U32 = mybir.dt.uint32
ALU = mybir.AluOpType
ACT = mybir.ActivationFunctionType
AX_X = mybir.AxisListType.X

P = 128
B, S, E = 2, 1024, 128
H = 16
D = E // H
N = B * S
NT = N // P
TABLE = 255
SCALE = float(E) ** -0.5
LN_EPS = 1e-5
NE, FF = 8, 512
CHUNK = 2 * N // NE
FC = FF // P

Q_PARTS = [0, 0, 0, 1, 1, 2]
K_PARTS = [0, 1, 2, 0, 1, 0]
ROWS = D * len(Q_PARTS)
MROWS = 3
HROWS = 64
PAIRS = H // 2

HALF = 512
GH = 4
NG = H // GH
KC = S // P
UNITS = B * (S // HALF) * NG
GROUP = 3
TILES = [(c, hh) for c in range(KC) for hh in range(GH)]
GROUPS = [TILES[i:i + GROUP] for i in range(0, len(TILES), GROUP)]
GPU = len(GROUPS)
RING = 4
ITER_UNITS = NG
ITERS = UNITS // ITER_UNITS
GPI = GPU * ITER_UNITS
ST = HALF // P
VW = 32
ROWF = E + 1
UNIT_DMAS = 7
ROUTE_UNIT = 1
ZROWS = 4
V_ITER = 17
CONST_STEPS = 21
SAFE = 36.0


def build(nc, x_rows, x_t, w_qkv_t, bias_toeplitz, bias_last, gamma, beta, wr_t, w1, w2, out):
    ctx = ExitStack()
    with ctx:
        def sb(name, shape, dt=F32):
            return ctx.enter_context(nc.sbuf_tensor(name, shape, dt))

        def psum(name, shape, dt=F32):
            return ctx.enter_context(nc.psum_tensor(name, shape, dt))

        def sem(name):
            return ctx.enter_context(nc.semaphore(name))

        q_op = nc.dram_tensor("q_op", (B, PAIRS, 2, ROWS, S), BF16, kind="Internal").ap()
        k_op = nc.dram_tensor("k_op", (B, PAIRS, 2, ROWS, S), BF16, kind="Internal").ap()
        m_op = nc.dram_tensor("m_op", (B, PAIRS, 2, MROWS, S), BF16, kind="Internal").ap()
        by_rank = nc.dram_tensor("by_rank", (NE * N, ROWF), F32, kind="Internal").ap()
        by_slot = nc.dram_tensor("by_slot", (2 * N, E), F32, kind="Internal").ap()

        qk_max = sb("qk_max", [P, 2])
        bound = sb("bound", [P, 1])
        head_bound = sb("head_bound", [1, H])
        bound_max = sb("bound_max", [1, 1])
        is_safe = sb("is_safe", [1, 1], I32)
        row_max = sb("row_max", [P, GH * KC])
        neg_max = sb("neg_max", [GH * KC, 2, P])
        max_part = sb("max_part", [GH * KC, MROWS, P], BF16)
        xt_sb = sb("xt_sb", [P, N])
        wqkv_sb = sb("wqkv_sb", [P, 3 * E])
        part = [sb(f"part{j}", [P, 2, N], BF16) for j in range(3)]
        resid = sb("resid", [P, 2, HALF])
        v_aug = sb("v_aug", [P, B * KC, H * VW])
        toep = sb("toep", [P, H, 2 * P])
        last_bc = sb("last_bc", [P, E])
        gamma_bc = sb("gamma_bc", [P, E])
        beta_bc = sb("beta_bc", [P, E])
        xb = sb("xb", [P, NT, E])
        wr_sb = sb("wr_sb", [P, NE])
        ident = sb("ident", [P, P])
        ones = sb("ones", [P, P])
        tri = sb("tri", [P, P], BF16)
        ones_bf = sb("ones_bf", [P, P], BF16)
        zero_rows = sb("zero_rows", [B * H * MROWS, S], BF16)
        zero_fill = sb("zero_fill", [P, ZROWS * ROWF])
        vsum = sb("vsum", [P, B, 3, E])
        ubase = sb("ubase", [P, B, 3, E])
        corr_t = sb("corr_t", [P, B * NG, 2 * P])
        bias_out = sb("bias_out", [P, NT, E])
        q_g = [sb(f"q_g{i}", [P, 2, HALF], BF16) for i in range(2)]
        k_g = [sb(f"k_g{i}", [P, 2, S], BF16) for i in range(2)]
        v_g = [sb(f"v_g{i}", [P, KC, GH * VW]) for i in range(2)]
        probs = sb("probs", [P, RING, GROUP, HALF])
        out_t = [sb(f"out_t{i}", [P, HALF]) for i in range(2)]
        rden = sb("rden", [P, ST, GH])
        attn = sb("attn", [P, ST, E])
        y_ln = sb("y_ln", [P, ST, E])
        stats = sb("stats", [P, NT, 6])
        mv = sb("mv", [P, NT, 2])
        rstd = sb("rstd", [P, NT])
        var_eps = sb("var_eps", [P, NT])
        expo = sb("expo", [P, NT])
        pay = [sb(f"pay{k}", [P, ST, ROWF]) for k in range(2)]
        ids = sb("ids", [P, 2, NT], I32)
        x1_all = sb("x1_all", [P, NT, E])
        x1_t = sb("x1_t", [P, HALF])
        logits = sb("logits", [P, ST, NE])
        top8 = sb("top8", [P, ST, 8])
        idx8 = sb("idx8", [P, ST, 8], U32)
        idx_f = sb("idx_f", [P, 2, ST])
        vals = sb("vals", [P, 2, NT])
        iota8 = sb("iota8", [P, ST, NE])
        onehot = sb("onehot", [P, 2, ST, NE])
        mask = sb("mask", [P, ST, NE], BF16)
        carry = sb("carry", [P, NE])
        carry_bf = sb("carry_bf", [P, NE], BF16)
        mask_sum = sb("mask_sum", [P, NE])
        picked = sb("picked", [P, 2, ST, NE])
        rank = sb("rank", [P, 2, ST])
        row_idx = sb("row_idx", [P, 2, ST], I32)
        counts = sb("counts", [P, NE])
        ends = sb("ends", [P, NE])
        skips = sb("skips", [P, NE])
        slot_f = sb("slot_f", [P, 4 * NE])
        slot_j = sb("slot_j", [P, 4 * NE])
        slot_add = sb("slot_add", [P, NE - 1, 4 * NE])
        slot_row = sb("slot_row", [P, 4 * NE], I32)
        w_pair = sb("w_pair", [P, 2, NT])
        e_gap = sb("e_gap", [P, NT])
        gap = sb("gap", [P, NT])
        act_spare = sb("act_spare", [P, 1])
        gidx = [sb(f"gidx{i}", [P, 4], I32) for i in range(2)]
        slot_to = sb("slot_to", [P, 4 * NE], I32)
        sidx = [sb(f"sidx{i}", [P, 4], I32) for i in range(2)]
        xg = [sb(f"xg{i}", [P, 4, ROWF]) for i in range(2)]
        w1_g = [sb(f"w1_g{i}", [P, FF]) for i in range(2)]
        w2_g = [sb(f"w2_g{i}", [P, FC, E]) for i in range(2)]
        xg_t = [xt_sb[:, i * CHUNK:(i + 1) * CHUNK] for i in range(2)]
        y_g = [xt_sb[:, (2 + i) * CHUNK:(3 + i) * CHUNK].rearrange("p (t d) -> p t d", d=E) for i in range(2)]
        y_t = resid[:, 0, :]
        h_t = [probs[:, 2 * i:2 * i + 2].rearrange("p r g n -> p (r g n)")[:, 0:FC * CHUNK]
               .rearrange("p (f n) -> p f n", f=FC) for i in range(2)]
        slots = v_aug[:].rearrange("p c n -> p (c n)")[:, 0:NT * 2 * E].rearrange("p (t n) -> p t n", t=NT)

        scores = [psum(f"scores{i}", [P, GROUP, HALF]) for i in range(2)]
        bank = [psum(f"bank{i}", [P, HALF]) for i in range(2)]

        const_step = sem("const_step")
        wx_loaded = [sem(f"wx_loaded{i}") for i in range(5)]
        aux_loaded = [sem(f"aux_loaded{i}") for i in range(6)]
        m_zeroed = sem("m_zeroed")
        rank_zeroed = sem("rank_zeroed")
        proj_ready = sem("proj_ready")
        part1_ready = sem("part1_ready")
        resid_ready = sem("resid_ready")
        part2_ready = sem("part2_ready")
        part3_ready = sem("part3_ready")
        batch_stored = sem("batch_stored")
        parts_stored = [sem(f"parts_stored{b}") for b in range(B)]
        bound_ready = sem("bound_ready")
        bound_turned = sem("bound_turned")
        safe_known = sem("safe_known")
        max_loaded = sem("max_loaded")
        max_scores = sem("max_scores")
        max_taken = sem("max_taken")
        max_turned = sem("max_turned")
        max_step = sem("max_step")
        max_split = sem("max_split")
        max_stored = sem("max_stored")
        v_ready = sem("v_ready")
        v_copied = sem("v_copied")
        vsum_ready = sem("vsum_ready")
        base_ready = sem("base_ready")
        corr_ready = sem("corr_ready")
        corr_copied = sem("corr_copied")
        corr_turned = sem("corr_turned")
        bias_ready = sem("bias_ready")
        xb_ready = sem("xb_ready")
        operands_loaded = [sem(f"operands_loaded{i}") for i in range(2)]
        scores_ready = sem("scores_ready")
        probs_ready = sem("probs_ready")
        unit_done = sem("unit_done")
        out_copied = sem("out_copied")
        out_turned = sem("out_turned")
        out_read = sem("out_read")
        v_step = sem("v_step")
        var_ready = sem("var_ready")
        rstd_ready = sem("rstd_ready")
        g_step = sem("g_step")
        x1_ready = sem("x1_ready")
        x1_turned = sem("x1_turned")
        x1_t_copied = sem("x1_t_copied")
        logits_ready = sem("logits_ready")
        mask_ready = sem("mask_ready")
        ranks_ready = sem("ranks_ready")
        ranks_read = sem("ranks_read")
        rows_ready = sem("rows_ready")
        rows_sent = sem("rows_sent")
        pay_free = sem("pay_free")
        counts_ready = sem("counts_ready")
        gap_ready = sem("gap_ready")
        e_ready = sem("e_ready")
        slots_known = sem("slots_known")
        w_loaded = [sem(f"w_loaded{i}") for i in range(2)]
        chunk_done = sem("chunk_done")
        gathered = [sem(f"gathered{i}") for i in range(2)]
        xg_turned = sem("xg_turned")
        xg_copied = sem("xg_copied")
        hidden_ready = sem("hidden_ready")
        gelu_done = sem("gelu_done")
        y_copied = sem("y_copied")
        y_turned = sem("y_turned")
        y_ready = sem("y_ready")
        slots_sent = [sem(f"slots_sent{i}") for i in range(2)]
        slots_loaded = [sem(f"slots_loaded{i}") for i in range(4)]
        out_ready = sem("out_ready")
        out_stored = sem("out_stored")

        settled = sem("settled")

        SETUP_SLOTS = [scores[i // 3][:, i % 3, :] for i in range(6)] + [bank[0][:], bank[1][:]]

        def settle(engine):
            engine.sem_inc(settled, 1)

        def piece(j, i):
            b, t, th = i // 4, i % 2, i // 2 % 2
            return part[j][:, t, b * S + th * HALF:b * S + (th + 1) * HALF]

        def store_part(engine, b, j):
            for t, op, parts in ((0, q_op, Q_PARTS), (1, k_op, K_PARTS)):
                for i in range(len(parts)):
                    if parts[i] == j:
                        engine.dma_start(op[b, :, :, i * D:(i + 1) * D, :].rearrange("p a d s -> (p a) d s"),
                                         part[j][:, t, b * S:(b + 1) * S]).then_inc(parts_stored[b], 16)

        block = ctx.enter_context(nc.Block())

        @block.sync
        def _(sp):
            sp.dma_start(wqkv_sb[:], w_qkv_t).then_inc(wx_loaded[4], 16)
            for i in range(4):
                cols = slice(i * HALF, (i + 1) * HALF)
                sp.dma_start(xt_sb[:, cols], x_t[:, cols]).then_inc(wx_loaded[i], 16)
            sp.dma_start(toep[:], bias_toeplitz).then_inc(aux_loaded[0], 16)
            sp.dma_start(last_bc[:], bias_last.broadcast_to([P, E])).then_inc(aux_loaded[4], 16)
            for j, ready in enumerate((part1_ready, part2_ready, part3_ready)):
                sp.wait_ge(ready, 4)
                store_part(sp, 0, j)
            sp.wait_ge(m_zeroed, 16)
            sp.wait_ge(parts_stored[0], 16 * 2 * len(Q_PARTS))
            sp.sem_inc(batch_stored, 1)
            sp.wait_ge(v_copied, 2)
            sp.wait_ge(const_step, CONST_STEPS)
            sp.wait_ge(safe_known, 1)
            with sp.If(sp.value_load(is_safe[:]) == 0):
                sp.wait_ge(batch_stored, 2)
                with sp.Fori(0, B) as b:
                    for g in range(NG):
                        for a in range(2):
                            rows = slice(a * HROWS, a * HROWS + ROWS)
                            for op, to in ((k_op, k_g[0]), (q_op, k_g[1])):
                                sp.dma_start(to[rows, :, :],
                                             op[bass.ds(b, 1), 2 * g:2 * g + 2, a].rearrange("o p r s -> r (o p) s")
                                             ).then_inc(max_loaded, 16)
                        sp.wait_ge(max_split, sp.snap(b * NG + g + 1))
                        for j in range(MROWS):
                            sp.dma_start(m_op[bass.ds(b, 1), 2 * g:2 * g + 2, :, j, :]
                                         .rearrange("o p a (t s) -> (o p a) t s", s=P),
                                         max_part[:, j, :]).then_inc(max_stored, 16)
                        sp.wait_ge(max_stored, sp.snap(b * (NG * MROWS * 16) + (g + 1) * MROWS * 16))
                    settle(sp)
            with sp.Fori(0, B) as b:
                sp.wait_ge(batch_stored, b + 1)
                settle(sp)
                with sp.Fori(0, S // HALF) as half:
                    for g in range(NG):
                        i = g % 2
                        sp.wait_ge(unit_done, sp.snap(b * (NG * S // HALF) + half * NG + g + 1))
                        qs = bass.ds(half * HALF, HALF)
                        for a in range(2):
                            rows = slice(a * HROWS, a * HROWS + ROWS)
                            mrows = slice(a * HROWS + ROWS, a * HROWS + ROWS + MROWS)
                            sp.dma_start(k_g[i][rows, :, :],
                                         k_op[bass.ds(b, 1), 2 * g:2 * g + 2, a].rearrange("o p r s -> r (o p) s")
                                         ).then_inc(operands_loaded[i], 16)
                            sp.dma_start(q_g[i][rows, :, :],
                                         q_op[bass.ds(b, 1), 2 * g:2 * g + 2, a, :, qs].rearrange("o p r s -> r (o p) s")
                                         ).then_inc(operands_loaded[i], 16)
                            sp.dma_start(q_g[i][mrows, :, :],
                                         m_op[bass.ds(b, 1), 2 * g:2 * g + 2, a, :, qs].rearrange("o p r s -> r (o p) s")
                                         ).then_inc(operands_loaded[i], 16)
                        sp.dma_start(v_g[i][:], v_aug[:, bass.ds(b * KC, KC), g * GH * VW:(g + 1) * GH * VW]
                                     ).then_inc(operands_loaded[i], 16)
            with sp.Fori(0, NE // 2) as c2:
                for i in range(2):
                    sp.wait_ge(chunk_done, sp.snap(c2 * 2 + i + 1))
                    sp.dma_start(w1_g[i][:], w1[bass.ds(c2 * 2 + i, 1)].rearrange("o d f -> d (o f)")
                                 ).then_inc(w_loaded[i], 16)
                    sp.dma_start(w2_g[i][:], w2[bass.ds(c2 * 2 + i, 1)].rearrange("o (c f) d -> f (o c) d", f=P)
                                 ).then_inc(w_loaded[i], 16)
            for i in range(2):
                sp.wait_ge(slots_sent[i], 64 * (NE // 2))
            slot_rows = by_slot.rearrange("(t p k) d -> p t (k d)", p=P, k=2)
            for i in range(4):
                sp.dma_start(slots[:, ST * i:ST * (i + 1), :], slot_rows[:, ST * i:ST * (i + 1), :]
                             ).then_inc(slots_loaded[i], 16)
            out_rows = out.rearrange("(t p) d -> p t d", p=P)
            for i in range(4):
                sp.wait_ge(out_ready, i + 1)
                sp.dma_start(out_rows[:, ST * i:ST * (i + 1), :], x1_all[:, ST * i:ST * (i + 1), :]
                             ).then_inc(out_stored, 16)
            sp.wait_ge(out_stored, 64)

        @block.gpsimd
        def _(pool):
            steps = [0]

            def step(ins):
                steps[0] += 1
                ins.then_inc(const_step, 1)

            step(nc.gpsimd.memset(zero_rows[:], 0.0))
            pool.wait_ge(const_step, 1)
            pool.dma_start(m_op.rearrange("b p a r s -> (b p a r) s"), zero_rows[:]).then_inc(m_zeroed, 16)
            step(nc.gpsimd.memset(ones[:], 1.0))
            step(nc.gpsimd.memset(ident[:], 0.0))
            step(nc.gpsimd.memset(ones_bf[:], 1.0))
            step(nc.gpsimd.memset(tri[:], 0.0))
            pool.wait_ge(const_step, 5)
            step(nc.gpsimd.affine_select(out=ident[:], in_=ident[:], compare_op=ALU.not_equal, fill=1.0, base=0,
                                         pattern=[[-1, P]], channel_multiplier=1))
            step(nc.gpsimd.affine_select(out=tri[:], in_=tri[:], compare_op=ALU.is_ge, fill=1.0, base=0,
                                         pattern=[[-1, P]], channel_multiplier=1))
            for i in range(2):
                step(nc.gpsimd.memset(q_g[i][:], 0.0))
                step(nc.gpsimd.memset(k_g[i][:], 1.0))
            va = v_aug[:].rearrange("p c (h w) -> p c h w", w=VW)
            step(nc.gpsimd.memset(va[:, 0:KC, :, D:VW], 0.0))
            step(nc.gpsimd.memset(va[:, KC:, :, D:VW], 0.0))
            pool.wait_ge(const_step, 13)
            step(nc.gpsimd.memset(va[:, :, :, D:D + 1], 1.0))
            step(nc.gpsimd.memset(expo[:], -0.5))
            step(nc.gpsimd.iota(iota8[:], pattern=[[0, ST], [1, NE]], base=0, channel_multiplier=0,
                                allow_small_or_imprecise_dtypes=True))
            step(nc.gpsimd.iota(ids[:], pattern=[[1, 2], [2 * P, NT]], base=0, channel_multiplier=2))
            step(nc.gpsimd.iota(slot_j[:], pattern=[[P, 4 * NE]], base=0, channel_multiplier=1,
                                allow_small_or_imprecise_dtypes=True))
            step(nc.gpsimd.memset(carry[:], 0.0))
            step(nc.gpsimd.memset(carry_bf[:], 0.0))
            step(nc.gpsimd.memset(zero_fill[:], 0.0))
            assert steps[0] == CONST_STEPS
            pool.wait_ge(const_step, CONST_STEPS)
            sp_parts = (part1_ready, part2_ready, part3_ready)
            for j in range(3):
                pool.wait_ge(sp_parts[j], 8)
                store_part(pool, 1, j)
            pool.wait_ge(parts_stored[1], 16 * 2 * len(Q_PARTS))
            pool.sem_inc(batch_stored, 1)
            pool.wait_ge(scores_ready, 1)
            pool.dma_start(xb[:], x_rows.rearrange("(t p) d -> p t d", p=P)).then_inc(aux_loaded[1], 16)
            pool.dma_start(gamma_bc[:], gamma.broadcast_to([P, E])).then_inc(aux_loaded[2], 16)
            pool.dma_start(beta_bc[:], beta.broadcast_to([P, E])).then_inc(aux_loaded[3], 16)
            fill = by_rank.rearrange("(p f r) d -> p f (r d)", p=P, r=ZROWS)
            n_fill = fill.shape[1]
            for i in range(4):
                pool.dma_start(fill[:, i * n_fill // 4:(i + 1) * n_fill // 4, :],
                               zero_fill[:].unsqueeze(1).broadcast_to([P, n_fill // 4, ZROWS * ROWF])
                               ).then_inc(rank_zeroed, 16)
            pool.wait_ge(aux_loaded[1], 16)
            pool.wait_ge(aux_loaded[3], 16)
            nc.gpsimd.tensor_tensor(xb[:], xb[:], beta_bc[:].unsqueeze(1).broadcast_to([P, NT, E]), ALU.add
                                    ).then_inc(xb_ready, 1)
            pool.sem_inc(pay_free, 1)

            g_steps = [0]

            def own(ins, base=0):
                g_steps[0] += 1
                ins.then_inc(g_step, 1)
                pool.wait_ge(g_step, base + g_steps[0])
                settle(pool)

            def inverse_roots(n, base):
                own(nc.gpsimd.tensor_scalar(var_eps[:, 0:n], mv[:, 0:n, 1], LN_EPS, None, ALU.add), base)
                nc.gpsimd.tensor_tensor(rstd[:, 0:n], var_eps[:, 0:n], expo[:, 0:n], ALU.pow).then_inc(rstd_ready, 1)

            G_ITER = 6
            with pool.Fori(0, ITERS) as it:
                base = pool.snap(it * G_ITER)
                for k in range(2):
                    pool.wait_ge(var_ready, pool.snap(it * 2 + k + 1))
                    settle(pool)
                    inverse_roots(ST, base)
                pool.wait_ge(x1_ready, pool.snap(it + 1))
                settle(pool)
                nc.gpsimd.tensor_copy(pay[1][:, :, 0:E], pay[0][:, :, 0:E])
                nc.gpsimd.tensor_copy(x1_all[:, bass.ds(it * ST, ST), :], pay[0][:, :, 0:E])
                for k in range(2):
                    own(nc.gpsimd.tensor_copy(pay[k][:, :, E:E + 1].bitcast(I32),
                                              ids[:, k, bass.ds(it * ST, ST)].unsqueeze(2)), base)
                pool.wait_ge(rank_zeroed, 64)
                pool.wait_ge(rows_ready, pool.snap(it + 1))
                settle(pool)
                for k in range(2):
                    for t in range(ST):
                        pool.indirect_dma_start(out=by_rank, in_=pay[k][:, t, :], in_offset=None,
                                                out_offset=bass.IndirectOffsetOnAxis(ap=row_idx[:, k, t:t + 1], axis=0)
                                                ).then_inc(rows_sent, 16)
                pool.wait_ge(rows_sent, pool.snap(it * (2 * ST * 16) + 2 * ST * 16))
                settle(pool)
                own(nc.gpsimd.memset(var_eps[:, ST:ST + 1], 0.0), base)
                own(nc.gpsimd.memset(var_eps[:, ST:ST + 1], 0.0), base)
                pool.sem_inc(pay_free, 1)
                assert g_steps[0] == G_ITER
            g_steps[0] = G_ITER * ITERS

            def gather(i):
                for t in range(4):
                    pool.indirect_dma_start(out=xg[i][:, t, :], out_offset=None, in_=by_rank,
                                            in_offset=bass.IndirectOffsetOnAxis(ap=gidx[i][:, t:t + 1], axis=0)
                                            ).then_inc(gathered[i], 16)

            def take_slots(i, c):
                return nc.gpsimd.tensor_copy(slot_to[:, bass.ds(c * 4, 4)].unsqueeze(2), xg[i][:, :, E:E + 1].bitcast(I32))

            def scatter(i, c):
                for t in range(4):
                    pool.indirect_dma_start(out=by_slot, in_=y_g[i][:, t, :], in_offset=None,
                                            out_offset=bass.IndirectOffsetOnAxis(ap=sidx[i][:, t:t + 1], axis=0)
                                            ).then_inc(slots_sent[i], 16)

            def work_off(i, c, base, turned=True, ahead=True):
                if turned:
                    pool.wait_ge(xg_turned, c + 2)
                    settle(pool)
                    ins = take_slots(1 - i, c + 1)
                    if ahead:
                        ins = nc.gpsimd.tensor_copy(gidx[1 - i][:], slot_row[:, bass.ds((c + 3) * 4, 4)])
                    own(ins, base)
                if ahead:
                    gather(1 - i)
                pool.wait_ge(y_ready, c + 1)
                settle(pool)
                own(nc.gpsimd.tensor_copy(sidx[i][:], slot_to[:, bass.ds(c * 4, 4)]), base)
                scatter(i, c)

            pool.wait_ge(slots_known, 1)
            nc.gpsimd.tensor_copy(gidx[0][:], slot_row[:, 0:4])
            own(nc.gpsimd.tensor_copy(gidx[1][:], slot_row[:, 4:8]))
            for i in range(2):
                gather(i)
            pool.wait_ge(xg_turned, 1)
            take_slots(0, 0)
            own(nc.gpsimd.tensor_copy(gidx[0][:], slot_row[:, 8:12]))
            gather(0)
            before = g_steps[0]
            with pool.Fori(0, NE // 2 - 2) as c2:
                base = pool.snap(c2 * 4)
                for i in range(2):
                    work_off(i, pool.snap(c2 * 2 + i), base)
                assert g_steps[0] == before + 4
            g_steps[0] = before + 4 * (NE // 2 - 2)
            for c in range(NE - 4, NE):
                work_off(c % 2, c, 0, turned=c + 1 < NE, ahead=c + 3 < NE)
            for i in range(4):
                pool.wait_ge(var_ready, 2 * ITERS + i + 1)
                sl = slice(ST * i, ST * (i + 1))
                own(nc.gpsimd.tensor_scalar(var_eps[:, sl], mv[:, sl, 1], LN_EPS, None, ALU.add))
                nc.gpsimd.tensor_tensor(rstd[:, sl], var_eps[:, sl], expo[:, sl], ALU.pow).then_inc(rstd_ready, 1)

        @block.scalar
        def _(act):
            act.dma_start(wr_sb[:], wr_t).then_inc(aux_loaded[5], 16)
            for i in range(9):
                if i < 8:
                    act.wait_ge(proj_ready, i + 1)
                    nc.scalar.copy(piece(0, i), SETUP_SLOTS[i]).then_inc(part1_ready, 1)
                if i > 0:
                    act.wait_ge(resid_ready, i)
                    nc.scalar.copy(piece(1, i - 1), resid[:, (i - 1) % 2, :]).then_inc(part2_ready, 1)
            for i in range(4):
                act.wait_ge(v_ready, i + 1)
                nc.scalar.copy(v_aug[:, 4 * i:4 * i + 4, :].rearrange("p c (h w) -> p c h w", w=VW)[:, :, :, 0:D],
                               SETUP_SLOTS[i].rearrange("p (c h d) -> p c h d", c=4, d=D)).then_inc(v_copied, 1)
            for n in range(B * NG):
                act.wait_ge(corr_ready, n + 1)
                nc.scalar.copy(corr_t[:, n, :], bank[n % 2][:, 0:2 * P]).then_inc(corr_copied, 1)
            with act.Fori(0, ITERS) as it:
                for n in range(GPI):
                    size = len(GROUPS[n % GPU])
                    act.wait_ge(scores_ready, act.snap(it * GPI + n + 1))
                    nc.scalar.activation(probs[:, n % RING, 0:size, :], scores[n % 2][:, 0:size, :], ACT.Exp,
                                         scale=SCALE).then_inc(probs_ready, 1)
            act.wait_ge(gap_ready, 1)
            nc.scalar.activation(e_gap[:], gap[:], ACT.Exp).then_inc(e_ready, 1)
            act.wait_ge(const_step, CONST_STEPS)
            nc.scalar.activation(act_spare[:], ones[:, 0:1], ACT.Gelu)
            with act.Fori(0, NE // 2) as c2:
                for i in range(2):
                    for f in range(FC):
                        act.wait_ge(hidden_ready, act.snap(c2 * (2 * FC) + i * FC + f + 1))
                        nc.scalar.activation(h_t[i][:, f, :], SETUP_SLOTS[f], ACT.Gelu).then_inc(gelu_done, 1)

        @block.tensor
        def _(pe):
            pe.sem_inc(unit_done, 2)
            pe.sem_inc(chunk_done, 2)
            pe.wait_ge(wx_loaded[4], 16)
            for i in range(8):
                b, t, th = i // 4, i % 2, i // 2 % 2
                if t == 0:
                    pe.wait_ge(wx_loaded[2 * b + th], 16)
                tok = b * S + th * HALF
                nc.tensor.matmul(SETUP_SLOTS[i], wqkv_sb[:, t * E:(t + 1) * E], xt_sb[:, tok:tok + HALF],
                                 start=True, stop=True).then_inc(proj_ready, 1)
            for i in range(4):
                pe.wait_ge(resid_ready, i + 1)
                for c in range(4):
                    tok = (4 * i + c) * P
                    last = nc.tensor.matmul(SETUP_SLOTS[i][:, c * E:(c + 1) * E], xt_sb[:, tok:tok + P],
                                            wqkv_sb[:, 2 * E:3 * E], start=True, stop=True)
                last.then_inc(v_ready, 1)
            pe.wait_ge(const_step, CONST_STEPS)
            pe.wait_ge(aux_loaded[0], 16)
            pe.wait_ge(aux_loaded[5], 16)
            pe.wait_ge(v_copied, 4)
            for b in range(B):
                for g in range(NG):
                    n = b * NG + g
                    if n == 0:
                        pe.wait_ge(resid_ready, 8)
                    if n == NG:
                        pe.wait_ge(bound_ready, 1)
                        nc.tensor.matmul(SETUP_SLOTS[4][0:1, 0:P], bound[:], ident[:], start=True, stop=True
                                         ).then_inc(bound_turned, 1)
                    if n >= 2:
                        pe.wait_ge(corr_copied, n - 1)
                    for hh in range(GH):
                        h = GH * g + hh
                        o = bank[n % 2][32 * hh:32 * hh + VW, :]
                        nc.tensor.matmul(o[:, 0:2 * P], v_aug[:, b * KC + KC - 1, h * VW:(h + 1) * VW], toep[:, h, :],
                                         start=True, stop=False)
                        last = nc.tensor.matmul(o[:, 0:P], v_aug[:, b * KC + KC - 2, h * VW:(h + 1) * VW],
                                                toep[:, h, P:2 * P], start=False, stop=True)
                    last.then_inc(corr_ready, 1)
            for b in range(B):
                pe.wait_ge(vsum_ready, b + 1)
                last = nc.tensor.matmul(SETUP_SLOTS[2 + 3 * b][:, 0:3 * E], ones[:],
                                        vsum[:, b].rearrange("p k e -> p (k e)"), start=True, stop=True)
            last.then_inc(base_ready, 1)
            for b in range(B):
                pe.wait_ge(corr_copied, NG * (b + 1))
                if b == 1:
                    pe.wait_ge(safe_known, 1)
                for g in range(NG):
                    for st in range(2):
                        last = nc.tensor.transpose(scores[b][:, st, g * P:(g + 1) * P],
                                                   corr_t[:, b * NG + g, st * P:(st + 1) * P], ident[:])
                last.then_inc(corr_turned, 1)
            pe.wait_ge(bias_ready, 2)

            def score_group(n, i, k, u):
                if k == 0:
                    pe.wait_ge(operands_loaded[i], u)
                for j, (c, hh) in enumerate(GROUPS[k]):
                    pair, a = hh // 2, hh % 2
                    rows = slice(a * HROWS, (a + 1) * HROWS)
                    last = nc.tensor.matmul(scores[n % 2][:, j, :], k_g[i][rows, pair, c * P:(c + 1) * P],
                                            q_g[i][rows, pair, :], start=True, stop=True)
                last.then_inc(scores_ready, 1)

            def value_group(n, i, k):
                for j, (c, hh) in enumerate(GROUPS[k]):
                    last = nc.tensor.matmul(bank[i][32 * hh:32 * hh + VW, :], v_g[i][:, c, hh * VW:(hh + 1) * VW],
                                            probs[:, n % RING, j, :], start=(c == 0), stop=(c == KC - 1))
                if k == GPU - 1:
                    last.then_inc(unit_done, 1)

            def turn_outputs(u, it, wait):
                i = u % 2
                pe.wait_ge(out_copied, wait)
                for st in range(ST):
                    last = nc.tensor.transpose(bank[i][:, st * P:(st + 1) * P], out_t[i][:, st * P:(st + 1) * P],
                                               ident[:])
                last.then_inc(out_turned, 1)

            def turn_x1(it, units_read):
                pe.wait_ge(x1_ready, it + 1)
                pe.wait_ge(out_read, units_read + 1)
                for t in range(ST):
                    last = nc.tensor.transpose(bank[0][:, t * P:(t + 1) * P], pay[0][:, t, 0:E], ident[:])
                last.then_inc(x1_turned, 1)

            def route_logits(it):
                pe.wait_ge(x1_t_copied, it + 1)
                for t in range(ST):
                    last = nc.tensor.matmul(bank[0][:, t * NE:(t + 1) * NE], x1_t[:, t * P:(t + 1) * P], wr_sb[:],
                                            start=True, stop=True)
                last.then_inc(logits_ready, 1)

            def route_ranks(it):
                pe.wait_ge(mask_ready, it + 1)
                for t in range(ST):
                    o = bank[0][:, t * NE:(t + 1) * NE]
                    nc.tensor.matmul(o, ones_bf[:], carry_bf[:], start=True, stop=False)
                    for s in range(t):
                        nc.tensor.matmul(o, ones_bf[:], mask[:, s, :], start=False, stop=False)
                    last = nc.tensor.matmul(o, tri[:], mask[:, t, :], start=False, stop=True)
                last.then_inc(ranks_ready, 1)

            def unit(u, it, hooks=(), ahead=True):
                i = u % 2
                hooks = dict(hooks)
                for k in range(GPU):
                    n = u * GPU + k
                    pe.wait_ge(probs_ready, it * GPI + n + 1)
                    if k + 2 < GPU:
                        score_group(n + 2, i, k + 2, None)
                    elif ahead:
                        nu = u + 1
                        score_group(n + 2, nu % 2, k + 2 - GPU,
                                    it * (UNIT_DMAS * 16 * 2) + UNIT_DMAS * 16 * (nu // 2 + 1))
                    if k == 0 and not (isinstance(it, int) and it == 0 and u == 0):
                        pe.wait_ge(out_read, it * ITER_UNITS + u)
                        if u == ROUTE_UNIT + 1:
                            pe.wait_ge(ranks_read, it + 1)
                    value_group(n, i, k)
                    if k == 2 and not (isinstance(it, int) and it == 0 and u == 0):
                        turn_outputs((u - 1) % ITER_UNITS, it, it * ITER_UNITS + u)
                    if k in hooks:
                        hooks[k]()

            with pe.If(pe.value_load(is_safe[:]) == 0):
                with pe.Fori(0, B * NG) as n:
                    pe.wait_ge(max_loaded, pe.snap(n * 64 + 64))
                    for j in range(GH * KC):
                        pair, a, st = j // KC // 2, j // KC % 2, j % KC
                        rows = slice(a * HROWS, a * HROWS + ROWS)
                        pe.wait_ge(max_taken, pe.snap(n * (GH * KC) + j + 1))
                        for c in range(2):
                            last = nc.tensor.matmul(scores[j % 2][:, c, :], k_g[1][rows, pair, st * P:(st + 1) * P],
                                                    k_g[0][rows, pair, c * HALF:(c + 1) * HALF], start=True, stop=True)
                        last.then_inc(max_scores, 1)
                    pe.wait_ge(max_taken, pe.snap(n * (GH * KC) + GH * KC + 2))
                    nc.tensor.transpose(bank[0][0:GH * KC, 0:P], row_max[:], ident[:]).then_inc(max_turned, 1)
            pe.wait_ge(operands_loaded[0], UNIT_DMAS * 16)
            for k in range(2):
                for_k = GROUPS[k]
                for j, (c, hh) in enumerate(for_k):
                    pair, a = hh // 2, hh % 2
                    rows = slice(a * HROWS, (a + 1) * HROWS)
                    last = nc.tensor.matmul(scores[k][:, j, :], k_g[0][rows, pair, c * P:(c + 1) * P],
                                            q_g[0][rows, pair, :], start=True, stop=True)
                last.then_inc(scores_ready, 1)
            unit(0, 0)
            unit(1, 0)
            with pe.Fori(0, ITERS - 1) as it_reg:
                it = pe.snap(it_reg)
                unit(2, it)
                unit(3, it)
                nxt = pe.snap(it_reg + 1)
                unit(0, nxt)
                unit(1, nxt, hooks={6: lambda: turn_x1(it, it * ITER_UNITS + ITER_UNITS + 1), 8: lambda: route_logits(it), 10: lambda: route_ranks(it)})
            unit(2, ITERS - 1)
            unit(3, ITERS - 1, ahead=False)
            turn_outputs(3, ITERS - 1, UNITS)
            turn_x1(ITERS - 1, UNITS)
            route_logits(ITERS - 1)
            route_ranks(ITERS - 1)
            pe.wait_ge(ranks_read, ITERS + 1)
            pe.wait_ge(rows_ready, ITERS)
            nc.tensor.matmul(bank[0][:, 0:NE], ones_bf[:], carry_bf[:], start=True, stop=True).then_inc(counts_ready, 1)

            def turn_rows(i, c, n):
                pe.wait_ge(gathered[i], n)
                for t in range(4):
                    last = nc.tensor.transpose(bank[i][:, t * P:(t + 1) * P], xg[i][:, t, 0:E], ident[:])
                last.then_inc(xg_turned, 1)

            def first_product(i, c, n):
                pe.wait_ge(w_loaded[i], n)
                pe.wait_ge(xg_copied, c + 1)
                for f in range(FC):
                    nc.tensor.matmul(SETUP_SLOTS[f], w1_g[i][:, f * P:(f + 1) * P], xg_t[i], start=True, stop=True
                                     ).then_inc(hidden_ready, 1)

            def second_product(i, c, n):
                pe.wait_ge(gelu_done, n)
                for f in range(FC):
                    last = nc.tensor.matmul(SETUP_SLOTS[4], w2_g[i][:, f, :], h_t[i][:, f, :],
                                            start=(f == 0), stop=(f == FC - 1))
                last.then_inc(chunk_done, 1)

            def turn_y(c):
                pe.wait_ge(y_copied, c + 1)
                for t in range(4):
                    last = nc.tensor.transpose(SETUP_SLOTS[5][:, t * P:(t + 1) * P], y_t[:, t * P:(t + 1) * P], ident[:])
                last.then_inc(y_turned, 1)

            def chunk(i, c, last=False):
                if not last:
                    n = 1 - i
                    turn_rows(n, c + 1, c * 32 + (64 + 32 * i))
                    second_product(i, c, c * FC + FC)
                    first_product(n, c + 1, c * 16 + (32 + 16 * i))
                else:
                    second_product(i, c, c * FC + FC)
                turn_y(c)

            pe.wait_ge(slots_known, 1)
            turn_rows(0, 0, 64)
            first_product(0, 0, 32)
            with pe.Fori(0, NE // 2 - 1) as c2:
                for i in range(2):
                    chunk(i, pe.snap(c2 * 2 + i))
            chunk(0, NE - 2)
            chunk(1, NE - 1, last=True)

        @block.vector
        def _(dve):
            dve.sem_inc(out_read, 1)
            dve.sem_inc(ranks_read, 1)
            steps = [0]

            def own(ins, base=0):
                steps[0] += 1
                ins.then_inc(v_step, 1)
                dve.wait_ge(v_step, base + steps[0])

            for i in range(9):
                if i < 8:
                    dve.wait_ge(part1_ready, i + 1)
                    if i >= 2:
                        dve.wait_ge(part3_ready, i - 1)
                    nc.vector.tensor_tensor(resid[:, i % 2, :], SETUP_SLOTS[i], piece(0, i), ALU.subtract
                                            ).then_inc(resid_ready, 1)
                if i > 0:
                    dve.wait_ge(part2_ready, i)
                    nc.vector.tensor_tensor(piece(2, i - 1), resid[:, (i - 1) % 2, :], piece(1, i - 1), ALU.subtract
                                            ).then_inc(part3_ready, 1)
            for t in range(2):
                ins = nc.vector.tensor_reduce(qk_max[:, t:t + 1], part[0][:, t, :], AX_X, ALU.max,
                                              apply_absolute_value=True)
            own(ins)
            nc.vector.tensor_tensor(bound[:], qk_max[:, 0:1], qk_max[:, 1:2], ALU.mult).then_inc(bound_ready, 1)
            dve.wait_ge(const_step, CONST_STEPS)
            for b in range(B):
                dve.wait_ge(v_copied, 2 * (b + 1))
                va = v_aug[:, b * KC:(b + 1) * KC, :].rearrange("p c (h w) -> p h w c", w=VW)
                vs = [vsum[:, b, k].rearrange("p (h d) -> p h d", d=D) for k in range(3)]
                own(nc.vector.tensor_reduce(vs[0], va[:, :, 0:D, 0:KC - 2], AX_X, ALU.add))
                own(nc.vector.tensor_tensor(vs[1], vs[0], va[:, :, 0:D, KC - 2], ALU.add))
                nc.vector.tensor_tensor(vs[2], vs[1], va[:, :, 0:D, KC - 1], ALU.add).then_inc(vsum_ready, 1)
            dve.wait_ge(bound_turned, 1)
            own(nc.vector.tensor_reduce(head_bound[:], SETUP_SLOTS[4][0:1, 0:P].rearrange("p (h d) -> p h d", d=D),
                                        AX_X, ALU.add))
            own(nc.vector.tensor_reduce(bound_max[:], head_bound[:], AX_X, ALU.max))
            nc.vector.tensor_scalar(is_safe[:], bound_max[:], SAFE / (SCALE * 1.01), None, ALU.is_le
                                    ).then_inc(safe_known, 1)
            dve.wait_ge(base_ready, 1)
            dve.wait_ge(aux_loaded[4], 16)
            for b in range(B):
                own(nc.vector.tensor_tensor(ubase[:, b], SETUP_SLOTS[2 + 3 * b][:, 0:3 * E].rearrange("p (k e) -> p k e", k=3),
                                            last_bc[:].unsqueeze(1).broadcast_to([P, 3, E]), ALU.mult))
            for b in range(B):
                o = b * KC
                own(nc.vector.tensor_copy(bias_out[:, o + 2:o + KC, :],
                                          ubase[:, b, 2:3, :].broadcast_to([P, KC - 2, E])))
                dve.wait_ge(corr_turned, b + 1)
                nc.vector.tensor_tensor(
                    bias_out[:, o:o + 2, :].rearrange("p t (h d) -> p t h d", d=D),
                    scores[b][:, 0:2, :].rearrange("p t (h w) -> p t h w", w=VW)[:, :, :, 0:D],
                    ubase[:, b, 0:2, :].rearrange("p t (h d) -> p t h d", d=D), ALU.add).then_inc(bias_ready, 1)

            dve.sem_inc(max_taken, 2)
            dve.wait_ge(safe_known, 1)
            with dve.If(dve.value_load(is_safe[:]) == 0):
                with dve.Fori(0, B * NG) as n:
                    for j in range(GH * KC):
                        dve.wait_ge(max_scores, dve.snap(n * (GH * KC) + j + 1))
                        nc.vector.tensor_reduce(row_max[:, j:j + 1], scores[j % 2][:, 0:2, :].rearrange("p c s -> p (c s)"),
                                                AX_X, ALU.max).then_inc(max_taken, 1)
                    dve.wait_ge(max_turned, dve.snap(n + 1))
                    nc.vector.tensor_scalar(neg_max[:, 0, :], bank[0][0:GH * KC, 0:P], -1.0, None, ALU.mult
                                            ).then_inc(max_step, 1)
                    dve.wait_ge(max_step, dve.snap(n * 4 + 1))
                    nc.vector.tensor_copy(max_part[:, 0, :], neg_max[:, 0, :]).then_inc(max_step, 1)
                    dve.wait_ge(max_step, dve.snap(n * 4 + 2))
                    nc.vector.tensor_tensor(neg_max[:, 1, :], neg_max[:, 0, :], max_part[:, 0, :], ALU.subtract
                                            ).then_inc(max_step, 1)
                    dve.wait_ge(max_step, dve.snap(n * 4 + 3))
                    nc.vector.tensor_copy(max_part[:, 1, :], neg_max[:, 1, :]).then_inc(max_step, 1)
                    dve.wait_ge(max_step, dve.snap(n * 4 + 4))
                    nc.vector.tensor_tensor(max_part[:, 2, :], neg_max[:, 1, :], max_part[:, 1, :], ALU.subtract
                                            ).then_inc(max_split, 1)

            def read_unit(u, it):
                i = u % 2
                dve.wait_ge(unit_done, it * ITER_UNITS + u + 3)
                nc.vector.tensor_copy(out_t[i][:], bank[i][:]).then_inc(out_copied, 1)
                dve.wait_ge(out_turned, it * ITER_UNITS + u + 1)
                turned = bank[i][:].rearrange("p (t h w) -> p t h w", t=ST, w=VW)
                own(nc.vector.reciprocal(rden[:], turned[:, :, :, D]), base[0])
                nc.vector.tensor_tensor(
                    attn[:, :, u * GH * D:(u + 1) * GH * D].rearrange("p t (h d) -> p t h d", d=D),
                    turned[:, :, :, 0:D], rden[:].unsqueeze(3).broadcast_to([P, ST, GH, D]), ALU.mult
                ).then_inc(out_read, 1)

            base = [0]

            def statistics(src, n, at=0):
                for t in range(n):
                    ins = nc.vector.bn_stats(stats[:, at + t, :], src(t))
                own(ins, base[0])
                settle(dve)
                for t in range(n):
                    ins = nc.vector.bn_aggr(mv[:, at + t, :], stats[:, at + t, :])
                ins.then_inc(var_ready, 1)

            def normalise(out_ap, src, n, at=0):
                for t in range(n):
                    ins = nc.vector.tensor_scalar(out_ap(t), src(t), mv[:, at + t, 0:1], rstd[:, at + t:at + t + 1],
                                                  ALU.subtract, ALU.mult)
                return ins

            def layer_norms(it):
                dve.wait_ge(out_read, it * ITER_UNITS + ITER_UNITS + 1)
                own(nc.vector.tensor_tensor(attn[:], attn[:], bias_out[:, bass.ds(it * ST, ST), :], ALU.add), base[0])
                statistics(lambda t: attn[:, t, :], ST)
                dve.wait_ge(rstd_ready, it * 2 + 1)
                own(normalise(lambda t: y_ln[:, t, :], lambda t: attn[:, t, :], ST), base[0])
                own(nc.vector.tensor_tensor(y_ln[:], y_ln[:], gamma_bc[:].unsqueeze(1).broadcast_to([P, ST, E]),
                                            ALU.mult), base[0])
                own(nc.vector.tensor_tensor(y_ln[:], y_ln[:], xb[:, bass.ds(it * ST, ST), :], ALU.add), base[0])
                statistics(lambda t: y_ln[:, t, :], ST)
                dve.wait_ge(rstd_ready, it * 2 + 2)
                dve.wait_ge(pay_free, it + 1)
                normalise(lambda t: pay[0][:, t, 0:E], lambda t: y_ln[:, t, :], ST).then_inc(x1_ready, 1)

            def route(it):
                dve.wait_ge(x1_turned, it + 1)
                nc.vector.tensor_copy(x1_t[:], bank[0][:]).then_inc(x1_t_copied, 1)
                dve.wait_ge(logits_ready, it + 1)
                own(nc.vector.tensor_copy(logits[:], bank[0][:, 0:ST * NE].rearrange("p (t e) -> p t e", e=NE)), base[0])
                settle(dve)
                for t in range(ST):
                    ins = nc.vector.max(top8[:, t, :], logits[:, t, :])
                own(ins, base[0])
                settle(dve)
                for t in range(ST):
                    ins = nc.vector.max_index(idx8[:, t, :], top8[:, t, :], logits[:, t, :])
                own(ins, base[0])
                nc.vector.tensor_copy(vals[:, :, bass.ds(it * ST, ST)], top8[:, :, 0:2].rearrange("p t k -> p k t"))
                own(nc.vector.tensor_copy(idx_f[:], idx8[:, :, 0:2].rearrange("p t k -> p k t")), base[0])
                for k in range(2):
                    ins = nc.vector.tensor_tensor(onehot[:, k], iota8[:],
                                                  idx_f[:, k].unsqueeze(2).broadcast_to([P, ST, NE]), ALU.is_equal)
                own(ins, base[0])
                nc.vector.tensor_tensor(mask[:], onehot[:, 0], onehot[:, 1], ALU.add).then_inc(mask_ready, 1)
                dve.wait_ge(ranks_ready, it + 1)
                ranks = bank[0][:, 0:ST * NE].rearrange("p (t e) -> p t e", e=NE)
                nc.vector.tensor_tensor(picked[:, 0], onehot[:, 0], ranks, ALU.mult)
                nc.vector.tensor_tensor(picked[:, 1], onehot[:, 1], ranks, ALU.mult).then_inc(ranks_read, 1)
                dve.wait_ge(ranks_read, it + 2)
                nc.vector.tensor_reduce(mask_sum[:], mask[:].rearrange("p t e -> p e t"), AX_X, ALU.add)
                own(nc.vector.tensor_reduce(rank[:], picked[:], AX_X, ALU.add), base[0])
                own(nc.vector.tensor_tensor(carry[:], carry[:], mask_sum[:], ALU.add), base[0])
                nc.vector.tensor_copy(carry_bf[:], carry[:])
                nc.vector.scalar_tensor_tensor(out=row_idx[:], in0=idx_f[:], scalar=float(N), in1=rank[:],
                                               op0=ALU.mult, op1=ALU.add).then_inc(rows_ready, 1)

            dve.wait_ge(aux_loaded[2], 16)
            dve.wait_ge(xb_ready, 1)
            read_unit(0, 0)
            before = steps[0]
            with dve.Fori(0, ITERS - 1) as it_reg:
                it = dve.snap(it_reg)
                base[0] = dve.snap(it_reg * V_ITER)
                read_unit(1, it)
                read_unit(2, it)
                read_unit(3, it)
                layer_norms(it)
                read_unit(0, dve.snap(it_reg + 1))
                route(it)
                assert steps[0] - before == V_ITER, steps[0] - before
            steps[0] = before + V_ITER * (ITERS - 1)
            base[0] = 0
            for u in range(1, 4):
                read_unit(u, ITERS - 1)
            layer_norms(ITERS - 1)
            route(ITERS - 1)

            dve.wait_ge(counts_ready, 1)
            own(nc.vector.tensor_copy(counts[:], bank[0][:, 0:NE]))
            own(nc.vector.tensor_tensor_scan(ends[:], counts[:], iota8[:, 0, :], 0.0, ALU.add, ALU.bypass))
            own(nc.vector.tensor_scalar(skips[:], counts[:], -1.0, float(N), ALU.mult, ALU.add))
            for e in range(NE - 1):
                ins = nc.vector.tensor_scalar(slot_add[:, e, :], slot_j[:], ends[:, e:e + 1], skips[:, e:e + 1],
                                              ALU.is_ge, ALU.mult)
            own(ins)
            own(nc.vector.tensor_reduce(slot_f[:], slot_add[:].rearrange("p e j -> p j e"), AX_X, ALU.add))
            nc.vector.tensor_tensor(slot_row[:], slot_f[:], slot_j[:], ALU.add).then_inc(slots_known, 1)
            nc.vector.tensor_tensor(gap[:], vals[:, 1], vals[:, 0], ALU.subtract).then_inc(gap_ready, 1)
            dve.wait_ge(e_ready, 1)
            own(nc.vector.tensor_scalar(gap[:], e_gap[:], 1.0, None, ALU.add))
            own(nc.vector.reciprocal(w_pair[:, 0], gap[:]))
            own(nc.vector.tensor_tensor(w_pair[:, 1], w_pair[:, 0], e_gap[:], ALU.mult))

            def copy_rows(i, c):
                dve.wait_ge(xg_turned, c + 1)
                nc.vector.tensor_copy(xg_t[i], bank[i][:]).then_inc(xg_copied, 1)

            def copy_y(i, c, first=False):
                dve.wait_ge(chunk_done, c + 3)
                nc.vector.tensor_copy(y_t, SETUP_SLOTS[4]).then_inc(y_copied, 1)
                dve.wait_ge(y_turned, c + 1)
                if not first:
                    dve.wait_ge(slots_sent[i], c * 32 - 32 * i)
                nc.vector.tensor_copy(y_g[i], SETUP_SLOTS[5].rearrange("p (t d) -> p t d", d=E)).then_inc(y_ready, 1)

            copy_rows(0, 0)
            for c in range(2):
                copy_rows(1 - c, c + 1)
                copy_y(c, c, first=True)
            with dve.Fori(1, NE // 2 - 1) as c2:
                for i in range(2):
                    c = dve.snap(c2 * 2 + i)
                    copy_rows(1 - i, dve.snap(c2 * 2 + i + 1))
                    copy_y(i, c)
            copy_rows(1, NE - 1)
            copy_y(0, NE - 2)
            copy_y(1, NE - 1)

            def tile_of(t):
                return x1_all[:, t, :]

            for q in range(4):
                dve.wait_ge(slots_loaded[q], 16)
                for k in range(2):
                    for t in range(ST * q, ST * (q + 1)):
                        ins = nc.vector.scalar_tensor_tensor(out=tile_of(t), in0=slots[:, t, k * E:(k + 1) * E],
                                                             scalar=w_pair[:, k, t:t + 1], in1=tile_of(t),
                                                             op0=ALU.mult, op1=ALU.add)
                    own(ins)
                statistics(lambda t: tile_of(ST * q + t), ST, ST * q)
            for q in range(4):
                dve.wait_ge(rstd_ready, 2 * ITERS + q + 1)
                normalise(lambda t: tile_of(ST * q + t), lambda t: tile_of(ST * q + t), ST, ST * q
                          ).then_inc(out_ready, 1)




_SHAPES = [("out_0_dram", (N, E))]


def kernel(**inputs):
    import concourse.bacc as bacc
    from concourse.bass_utils import run_bass_kernel_spmd as run

    nc = bacc.Bacc("TRN2", target_bir_lowering=False, num_devices=1)
    x = np.asarray(inputs["L0_attn_x"]).reshape(N, E)
    table = np.asarray(inputs["L0_attn_bias_table"])
    rows = np.minimum(P - 1 + np.arange(2 * P)[None, :] - np.arange(P)[:, None], TABLE - 1)
    arrays = {
        "x_rows": x,
        "x_t": x.T,
        "w_qkv_t": np.concatenate([np.asarray(inputs[f"L0_attn_W{w}"]).T for w in "qkv"], axis=1),
        "bias_toeplitz": table[rows].transpose(0, 2, 1),
        "bias_last": np.repeat(table[TABLE - 1], D)[None, :],
        "gamma": np.asarray(inputs["L0_attn_ln_gamma"])[None, :],
        "beta": np.asarray(inputs["L0_attn_ln_beta"])[None, :],
        "wr_t": np.asarray(inputs["L0_ffn_Wr"]).T,
        "w1": np.asarray(inputs["L0_ffn_W1"]),
        "w2": np.asarray(inputs["L0_ffn_W2"]),
    }
    arrays = {f"in_{n}": np.ascontiguousarray(a) for n, a in arrays.items()}
    args = [nc.dram_tensor(n, a.shape, mybir.dt.from_np(a.dtype), kind="ExternalInput").ap() for n, a in arrays.items()]
    out = nc.dram_tensor("out_y", (N, E), F32, kind="ExternalOutput").ap()
    build(nc, *args, out)
    r = run(nc, [arrays], core_ids=[0])
    return r.results[0]["out_y"].reshape(B, S, E)
```

```python
from contextlib import ExitStack

import numpy as np

import concourse.bass as bass
from concourse import mybir

F32 = mybir.dt.float32
BF16 = mybir.dt.bfloat16
I32 = mybir.dt.int32
U32 = mybir.dt.uint32
ALU = mybir.AluOpType
ACT = mybir.ActivationFunctionType
AX_X = mybir.AxisListType.X

P = 128
B, S, E = 2, 1024, 128
H = 16
D = E // H
N = B * S
NT = N // P
TABLE = 255
SCALE = float(E) ** -0.5
LN_EPS = 1e-5
NE, FF = 8, 512
CHUNK = 2 * N // NE
FC = FF // P

Q_PARTS = [0, 0, 0, 1, 1, 2]
K_PARTS = [0, 1, 2, 0, 1, 0]
ROWS = D * len(Q_PARTS)
MROWS = 3
HROWS = 64
KROWS = ROWS + MROWS
PAIRS = H // 2

HALF = 512
GH = 4
NG = H // GH
KC = S // P
UNITS = B * (S // HALF) * NG
GROUP = 3
TILES = [(c, hh) for c in range(KC) for hh in range(GH)]
GROUPS = [TILES[i:i + GROUP] for i in range(0, len(TILES), GROUP)]
GPU = len(GROUPS)
RING = 4
ITER_UNITS = NG
ITERS = UNITS // ITER_UNITS
GPI = GPU * ITER_UNITS
ST = HALF // P
VW = 32
ROWF = E + 1
UNIT_DMAS = 5
ROUTE_UNIT = 1
ZROWS = 4
V_ITER = 15
CONST_STEPS = 22
SAFE = 36.0


def build(nc, x_rows, x_t, w_qkv_t, bias_toeplitz, bias_last, gamma, beta, wr_t, w1, w2, out):
    ctx = ExitStack()
    with ctx:
        def sb(name, shape, dt=F32):
            return ctx.enter_context(nc.sbuf_tensor(name, shape, dt))

        def psum(name, shape, dt=F32):
            return ctx.enter_context(nc.psum_tensor(name, shape, dt))

        def sem(name):
            return ctx.enter_context(nc.semaphore(name))

        q_op = nc.dram_tensor("q_op", (B, PAIRS, 2, KROWS, S), BF16, kind="Internal").ap()
        k_op = nc.dram_tensor("k_op", (B, PAIRS, 2, KROWS, S), BF16, kind="Internal").ap()
        by_rank = nc.dram_tensor("by_rank", (NE * N, ROWF), F32, kind="Internal").ap()
        by_slot = nc.dram_tensor("by_slot", (2 * N, E), F32, kind="Internal").ap()

        qk_max = sb("qk_max", [P, 2])
        bound = sb("bound", [P, 1])
        head_bound = sb("head_bound", [1, H])
        bound_max = sb("bound_max", [1, 1])
        is_safe = sb("is_safe", [1, 1], I32)
        row_max = sb("row_max", [P, GH * KC])
        neg_max = sb("neg_max", [GH * KC, 2, P])
        max_part = sb("max_part", [GH * KC, MROWS, P], BF16)
        xt_sb = sb("xt_sb", [P, N])
        wqkv_sb = sb("wqkv_sb", [P, 3 * E])
        part = [sb(f"part{j}", [P, 2, N], BF16) for j in range(3)]
        resid = sb("resid", [P, 2, HALF])
        v_aug = sb("v_aug", [P, B * KC, H * VW])
        toep = sb("toep", [P, H, 2 * P])
        last_bc = sb("last_bc", [P, E])
        gamma_bc = sb("gamma_bc", [P, E])
        beta_bc = sb("beta_bc", [P, E])
        xb = sb("xb", [P, NT, E])
        wr_sb = sb("wr_sb", [P, NE])
        wr_c = sb("wr_c", [P, NE])
        ident = sb("ident", [P, P])
        ones = sb("ones", [P, P])
        tri = sb("tri", [P, P], BF16)
        ones_bf = sb("ones_bf", [P, P], BF16)
        pad_rows = sb("pad_rows", [B * PAIRS * 2, 2, HALF], BF16)
        zero_fill = sb("zero_fill", [P, ZROWS * ROWF])
        vsum = sb("vsum", [P, B, 3, E])
        ubase = sb("ubase", [P, B, 3, E])
        corr_t = sb("corr_t", [P, B * NG, 2 * P])
        bias_out = sb("bias_out", [P, NT, E])
        q_g = [sb(f"q_g{i}", [P, 2, HALF], BF16) for i in range(2)]
        k_g = [sb(f"k_g{i}", [P, 2, S], BF16) for i in range(2)]
        v_g = [sb(f"v_g{i}", [P, KC, GH * VW]) for i in range(2)]
        probs = sb("probs", [P, RING, GROUP, HALF])
        out_t = [sb(f"out_t{i}", [P, HALF]) for i in range(2)]
        rden = sb("rden", [P, ST, GH])
        attn = sb("attn", [P, ST, E])
        y_ln = sb("y_ln", [P, ST, E])
        stats = sb("stats", [P, NT, 6])
        mv = sb("mv", [P, NT, 2])
        rstd = sb("rstd", [P, NT])
        var_eps = sb("var_eps", [P, NT])
        shift = sb("shift", [P, NT])
        expo = sb("expo", [P, NT])
        pay = [sb(f"pay{k}", [P, ST, ROWF]) for k in range(2)]
        ids = sb("ids", [P, 2, NT], I32)
        x1_all = sb("x1_all", [P, NT, E])
        y_ln_t = sb("y_ln_t", [P, HALF])
        logits = sb("logits", [P, ST, NE])
        top8 = sb("top8", [P, ST, 8])
        idx8 = sb("idx8", [P, ST, 8], U32)
        idx_f = sb("idx_f", [P, 2, ST])
        vals = sb("vals", [P, 2, NT])
        iota8 = sb("iota8", [P, ST, NE])
        onehot = sb("onehot", [P, 2, ST, NE])
        mask = sb("mask", [P, ST, NE], BF16)
        carry = sb("carry", [P, NE])
        carry_bf = sb("carry_bf", [P, NE], BF16)
        mask_sum = sb("mask_sum", [P, NE])
        picked = sb("picked", [P, 2, ST, NE])
        rank = sb("rank", [P, 2, ST])
        row_idx = sb("row_idx", [P, 2, ST], I32)
        counts = sb("counts", [P, NE])
        ends = sb("ends", [P, NE])
        skips = sb("skips", [P, NE])
        slot_f = sb("slot_f", [P, 4 * NE])
        slot_j = sb("slot_j", [P, 4 * NE])
        slot_add = sb("slot_add", [P, NE - 1, 4 * NE])
        slot_row = sb("slot_row", [P, 4 * NE], I32)
        w_pair = sb("w_pair", [P, 2, NT])
        e_gap = sb("e_gap", [P, NT])
        gap = sb("gap", [P, NT])
        act_spare = sb("act_spare", [P, 1])
        gidx = [sb(f"gidx{i}", [P, 4], I32) for i in range(2)]
        slot_to = sb("slot_to", [P, 4 * NE], I32)
        sidx = [sb(f"sidx{i}", [P, 4], I32) for i in range(2)]
        xg = [sb(f"xg{i}", [P, 4, ROWF]) for i in range(2)]
        w1_g = [sb(f"w1_g{i}", [P, FF]) for i in range(2)]
        w2_g = [sb(f"w2_g{i}", [P, FC, E]) for i in range(2)]
        max_k, max_q = part[1][:, :, 0:S], part[2][:, :, 0:S]
        xg_t = [xt_sb[:, i * CHUNK:(i + 1) * CHUNK] for i in range(2)]
        y_g = [xt_sb[:, (2 + i) * CHUNK:(3 + i) * CHUNK].rearrange("p (t d) -> p t d", d=E) for i in range(2)]
        y_t = resid[:, 0, :]
        h_t = [probs[:, 2 * i:2 * i + 2].rearrange("p r g n -> p (r g n)")[:, 0:FC * CHUNK]
               .rearrange("p (f n) -> p f n", f=FC) for i in range(2)]
        slots = v_aug[:].rearrange("p c n -> p (c n)")[:, 0:NT * 2 * E].rearrange("p (t n) -> p t n", t=NT)

        scores = [psum(f"scores{i}", [P, GROUP, HALF]) for i in range(2)]
        bank = [psum(f"bank{i}", [P, HALF]) for i in range(2)]

        const_step = sem("const_step")
        wx_loaded = [sem(f"wx_loaded{i}") for i in range(5)]
        aux_loaded = [sem(f"aux_loaded{i}") for i in range(6)]
        pads_stored = sem("pads_stored")
        rank_zeroed = sem("rank_zeroed")
        proj_ready = sem("proj_ready")
        part1_ready = sem("part1_ready")
        resid_ready = sem("resid_ready")
        part2_ready = sem("part2_ready")
        part3_ready = sem("part3_ready")
        batch_stored = sem("batch_stored")
        parts_stored = [sem(f"parts_stored{b}") for b in range(B)]
        bound_ready = sem("bound_ready")
        bound_turned = sem("bound_turned")
        safe_known = sem("safe_known")
        max_loaded = sem("max_loaded")
        max_scores = sem("max_scores")
        max_taken = sem("max_taken")
        max_turned = sem("max_turned")
        max_step = sem("max_step")
        max_split = sem("max_split")
        max_stored = sem("max_stored")
        maxima_known = sem("maxima_known")
        v_ready = sem("v_ready")
        v_copied = sem("v_copied")
        vsum_ready = sem("vsum_ready")
        base_ready = sem("base_ready")
        corr_ready = sem("corr_ready")
        corr_copied = sem("corr_copied")
        corr_turned = sem("corr_turned")
        bias_ready = sem("bias_ready")
        wr_centred = sem("wr_centred")
        xb_ready = sem("xb_ready")
        operands_loaded = [sem(f"operands_loaded{i}") for i in range(2)]
        scores_ready = sem("scores_ready")
        probs_ready = sem("probs_ready")
        unit_done = sem("unit_done")
        out_copied = sem("out_copied")
        out_turned = sem("out_turned")
        out_read = sem("out_read")
        v_step = sem("v_step")
        var_ready = sem("var_ready")
        rstd_ready = sem("rstd_ready")
        g_step = sem("g_step")
        x1_ready = sem("x1_ready")
        y_ln_ready = sem("y_ln_ready")
        y_ln_turned = sem("y_ln_turned")
        y_ln_t_copied = sem("y_ln_t_copied")
        logits_ready = sem("logits_ready")
        mask_ready = sem("mask_ready")
        ranks_ready = sem("ranks_ready")
        ranks_read = sem("ranks_read")
        rows_ready = sem("rows_ready")
        rows_sent = sem("rows_sent")
        pay_free = sem("pay_free")
        counts_ready = sem("counts_ready")
        gap_ready = sem("gap_ready")
        e_ready = sem("e_ready")
        slots_known = sem("slots_known")
        w_loaded = [sem(f"w_loaded{i}") for i in range(2)]
        chunk_done = sem("chunk_done")
        gathered = [sem(f"gathered{i}") for i in range(2)]
        xg_turned = sem("xg_turned")
        xg_copied = sem("xg_copied")
        hidden_ready = sem("hidden_ready")
        gelu_done = sem("gelu_done")
        y_copied = sem("y_copied")
        y_turned = sem("y_turned")
        y_ready = sem("y_ready")
        slots_sent = [sem(f"slots_sent{i}") for i in range(2)]
        slots_loaded = [sem(f"slots_loaded{i}") for i in range(4)]
        shift_ready = sem("shift_ready")
        weights_ready = sem("weights_ready")
        slot0_weighted = sem("slot0_weighted")
        slot0_added = sem("slot0_added")
        out_ready = sem("out_ready")
        last_ready = sem("last_ready")
        out_stored = sem("out_stored")

        settled = sem("settled")

        SETUP_SLOTS = [scores[i // 3][:, i % 3, :] for i in range(6)] + [bank[0][:], bank[1][:]]

        def settle(engine):
            engine.sem_inc(settled, 1)

        def piece(j, i):
            b, t, th = i // 4, i % 2, i // 2 % 2
            return part[j][:, t, b * S + th * HALF:b * S + (th + 1) * HALF]

        def store_part(engine, b, j):
            for t, op, parts in ((0, q_op, Q_PARTS), (1, k_op, K_PARTS)):
                for i in range(len(parts)):
                    if parts[i] == j:
                        engine.dma_start(op[b, :, :, i * D:(i + 1) * D, :].rearrange("p a d s -> (p a) d s"),
                                         part[j][:, t, b * S:(b + 1) * S]).then_inc(parts_stored[b], 16)

        block = ctx.enter_context(nc.Block())

        @block.sync
        def _(sp):
            sp.dma_start(wqkv_sb[:], w_qkv_t).then_inc(wx_loaded[4], 16)
            for i in range(4):
                cols = slice(i * HALF, (i + 1) * HALF)
                sp.dma_start(xt_sb[:, cols], x_t[:, cols]).then_inc(wx_loaded[i], 16)
            sp.dma_start(toep[:], bias_toeplitz).then_inc(aux_loaded[0], 16)
            sp.dma_start(last_bc[:], bias_last.broadcast_to([P, E])).then_inc(aux_loaded[4], 16)
            for j, ready in enumerate((part1_ready, part2_ready, part3_ready)):
                sp.wait_ge(ready, 4)
                store_part(sp, 0, j)
            sp.wait_ge(pads_stored, 32)
            sp.wait_ge(parts_stored[0], 16 * 2 * len(Q_PARTS))
            sp.sem_inc(batch_stored, 1)
            sp.wait_ge(v_copied, 2)
            sp.wait_ge(const_step, CONST_STEPS)
            with sp.Fori(0, B) as b:
                sp.wait_ge(batch_stored, b + 1)
                settle(sp)
                with sp.Fori(0, S // HALF) as half:
                    for g in range(NG):
                        i = g % 2
                        sp.wait_ge(unit_done, sp.snap(b * (NG * S // HALF) + half * NG + g + 1))
                        qs = bass.ds(half * HALF, HALF)
                        for a in range(2):
                            rows = slice(a * HROWS, a * HROWS + KROWS)
                            sp.dma_start(k_g[i][rows, :, :], k_op[bass.ds(b, 1), 2 * g:2 * g + 2, a]
                                         .rearrange("o p r s -> r (o p) s")).then_inc(operands_loaded[i], 16)
                            sp.dma_start(q_g[i][rows, :, :], q_op[bass.ds(b, 1), 2 * g:2 * g + 2, a, :, qs]
                                         .rearrange("o p r s -> r (o p) s")).then_inc(operands_loaded[i], 16)
                        sp.dma_start(v_g[i][:], v_aug[:, bass.ds(b * KC, KC), g * GH * VW:(g + 1) * GH * VW]
                                     ).then_inc(operands_loaded[i], 16)
            with sp.Fori(0, NE // 2) as c2:
                for i in range(2):
                    sp.wait_ge(chunk_done, sp.snap(c2 * 2 + i + 1))
                    sp.dma_start(w1_g[i][:], w1[bass.ds(c2 * 2 + i, 1)].rearrange("o d f -> d (o f)")
                                 ).then_inc(w_loaded[i], 16)
                    sp.dma_start(w2_g[i][:], w2[bass.ds(c2 * 2 + i, 1)].rearrange("o (c f) d -> f (o c) d", f=P)
                                 ).then_inc(w_loaded[i], 16)
            for i in range(2):
                sp.wait_ge(slots_sent[i], 64 * (NE // 2))
            slot_rows = by_slot.rearrange("(t p k) d -> p t (k d)", p=P, k=2)
            for i in range(4):
                sp.dma_start(slots[:, ST * i:ST * (i + 1), :], slot_rows[:, ST * i:ST * (i + 1), :]
                             ).then_inc(slots_loaded[i], 16)
            out_rows = out.rearrange("(t p) d -> p t d", p=P)
            for i in range(4):
                sp.wait_ge(out_ready, i + 1)
                if i == 3:
                    sp.wait_ge(last_ready, 1)
                sp.dma_start(out_rows[:, ST * i:ST * (i + 1), :], x1_all[:, ST * i:ST * (i + 1), :]
                             ).then_inc(out_stored, 16)
            sp.wait_ge(out_stored, 64)

        @block.gpsimd
        def _(pool):
            steps = [0]

            def step(ins):
                steps[0] += 1
                ins.then_inc(const_step, 1)

            step(nc.gpsimd.memset(pad_rows[:, 0, :], 0.0))
            step(nc.gpsimd.memset(pad_rows[:, 1, :], 1.0))
            pool.wait_ge(const_step, 2)
            for i, op in enumerate((q_op, k_op)):
                pool.dma_start(op.rearrange("b p a r s -> (b p a) r s")[:, ROWS:KROWS, :]
                               .rearrange("x r (h s) -> x (r h) s", s=HALF),
                               pad_rows[:, i:i + 1, :].broadcast_to([B * PAIRS * 2, MROWS * S // HALF, HALF])
                               ).then_inc(pads_stored, 16)
            step(nc.gpsimd.memset(ones[:], 1.0))
            step(nc.gpsimd.memset(ident[:], 0.0))
            step(nc.gpsimd.memset(ones_bf[:], 1.0))
            step(nc.gpsimd.memset(tri[:], 0.0))
            pool.wait_ge(const_step, 6)
            step(nc.gpsimd.affine_select(out=ident[:], in_=ident[:], compare_op=ALU.not_equal, fill=1.0, base=0,
                                         pattern=[[-1, P]], channel_multiplier=1))
            step(nc.gpsimd.affine_select(out=tri[:], in_=tri[:], compare_op=ALU.is_ge, fill=1.0, base=0,
                                         pattern=[[-1, P]], channel_multiplier=1))
            for i in range(2):
                step(nc.gpsimd.memset(q_g[i][:], 0.0))
                step(nc.gpsimd.memset(k_g[i][:], 0.0))
            va = v_aug[:].rearrange("p c (h w) -> p c h w", w=VW)
            step(nc.gpsimd.memset(va[:, 0:KC, :, D:VW], 0.0))
            step(nc.gpsimd.memset(va[:, KC:, :, D:VW], 0.0))
            pool.wait_ge(const_step, 14)
            step(nc.gpsimd.memset(va[:, :, :, D:D + 1], 1.0))
            step(nc.gpsimd.memset(expo[:], -0.5))
            step(nc.gpsimd.iota(iota8[:], pattern=[[0, ST], [1, NE]], base=0, channel_multiplier=0,
                                allow_small_or_imprecise_dtypes=True))
            step(nc.gpsimd.iota(ids[:], pattern=[[1, 2], [2 * P, NT]], base=0, channel_multiplier=2))
            step(nc.gpsimd.iota(slot_j[:], pattern=[[P, 4 * NE]], base=0, channel_multiplier=1,
                                allow_small_or_imprecise_dtypes=True))
            step(nc.gpsimd.memset(carry[:], 0.0))
            step(nc.gpsimd.memset(carry_bf[:], 0.0))
            step(nc.gpsimd.memset(zero_fill[:], 0.0))
            assert steps[0] == CONST_STEPS
            pool.wait_ge(const_step, CONST_STEPS)
            pool.wait_ge(bias_ready, 2)
            for j, ready in enumerate((part1_ready, part2_ready, part3_ready)):
                pool.wait_ge(ready, 8)
                store_part(pool, 1, j)
            pool.wait_ge(parts_stored[1], 16 * 2 * len(Q_PARTS))
            pool.sem_inc(batch_stored, 1)
            pool.dma_start(xb[:], x_rows.rearrange("(t p) d -> p t d", p=P)).then_inc(aux_loaded[1], 16)
            pool.dma_start(gamma_bc[:], gamma.broadcast_to([P, E])).then_inc(aux_loaded[2], 16)
            pool.dma_start(beta_bc[:], beta.broadcast_to([P, E])).then_inc(aux_loaded[3], 16)
            pool.wait_ge(aux_loaded[1], 16)
            pool.wait_ge(aux_loaded[3], 16)
            nc.gpsimd.tensor_tensor(xb[:], xb[:], beta_bc[:].unsqueeze(1).broadcast_to([P, NT, E]), ALU.add
                                    ).then_inc(xb_ready, 1)
            fill = by_rank.rearrange("(p f r) d -> p f (r d)", p=P, r=ZROWS)
            n_fill = fill.shape[1]
            for i in range(2):
                pool.wait_ge(operands_loaded[i], 2 * UNIT_DMAS * 16)
                pool.dma_start(fill[:, i * n_fill // 2:(i + 1) * n_fill // 2, :],
                               zero_fill[:].unsqueeze(1).broadcast_to([P, n_fill // 2, ZROWS * ROWF])
                               ).then_inc(rank_zeroed, 16)
            pool.sem_inc(pay_free, 1)

            g_steps = [0]

            def own(ins, base=0):
                g_steps[0] += 1
                ins.then_inc(g_step, 1)
                pool.wait_ge(g_step, base + g_steps[0])
                settle(pool)

            def inverse_roots(n, base):
                own(nc.gpsimd.tensor_scalar(var_eps[:, 0:n], mv[:, 0:n, 1], LN_EPS, None, ALU.add), base)
                nc.gpsimd.tensor_tensor(rstd[:, 0:n], var_eps[:, 0:n], expo[:, 0:n], ALU.pow).then_inc(rstd_ready, 1)

            G_ITER = 5
            with pool.Fori(0, ITERS) as it:
                base = pool.snap(it * G_ITER)
                for k in range(2):
                    pool.wait_ge(var_ready, pool.snap(it * 2 + k + 1))
                    settle(pool)
                    inverse_roots(ST, base)
                pool.wait_ge(x1_ready, pool.snap(it + 1))
                settle(pool)
                nc.gpsimd.tensor_copy(pay[1][:, :, 0:E], pay[0][:, :, 0:E])
                for k in range(2):
                    own(nc.gpsimd.tensor_copy(pay[k][:, :, E:E + 1].bitcast(I32),
                                              ids[:, k, bass.ds(it * ST, ST)].unsqueeze(2)), base)
                pool.wait_ge(rank_zeroed, 32)
                pool.wait_ge(rows_ready, pool.snap(it + 1))
                settle(pool)
                for k in range(2):
                    for t in range(ST):
                        pool.indirect_dma_start(out=by_rank, in_=pay[k][:, t, :], in_offset=None,
                                                out_offset=bass.IndirectOffsetOnAxis(ap=row_idx[:, k, t:t + 1], axis=0)
                                                ).then_inc(rows_sent, 16)
                own(nc.gpsimd.tensor_copy(x1_all[:, bass.ds(it * ST, ST), :], pay[0][:, :, 0:E]), base)
                pool.wait_ge(rows_sent, pool.snap(it * (2 * ST * 16) + 2 * ST * 16))
                pool.sem_inc(pay_free, 1)
                assert g_steps[0] == G_ITER
            g_steps[0] = G_ITER * ITERS

            def gather(i):
                for t in range(4):
                    pool.indirect_dma_start(out=xg[i][:, t, :], out_offset=None, in_=by_rank,
                                            in_offset=bass.IndirectOffsetOnAxis(ap=gidx[i][:, t:t + 1], axis=0)
                                            ).then_inc(gathered[i], 16)

            def take_slots(i, c):
                return nc.gpsimd.tensor_copy(slot_to[:, bass.ds(c * 4, 4)].unsqueeze(2), xg[i][:, :, E:E + 1].bitcast(I32))

            def scatter(i, c):
                for t in range(4):
                    pool.indirect_dma_start(out=by_slot, in_=y_g[i][:, t, :], in_offset=None,
                                            out_offset=bass.IndirectOffsetOnAxis(ap=sidx[i][:, t:t + 1], axis=0)
                                            ).then_inc(slots_sent[i], 16)

            def work_off(i, c, base, turned=True, ahead=True):
                if turned:
                    pool.wait_ge(xg_turned, c + 2)
                    settle(pool)
                    ins = take_slots(1 - i, c + 1)
                    if ahead:
                        ins = nc.gpsimd.tensor_copy(gidx[1 - i][:], slot_row[:, bass.ds((c + 3) * 4, 4)])
                    own(ins, base)
                if ahead:
                    gather(1 - i)
                pool.wait_ge(y_ready, c + 1)
                settle(pool)
                own(nc.gpsimd.tensor_copy(sidx[i][:], slot_to[:, bass.ds(c * 4, 4)]), base)
                scatter(i, c)

            pool.wait_ge(slots_known, 1)
            nc.gpsimd.tensor_copy(gidx[0][:], slot_row[:, 0:4])
            own(nc.gpsimd.tensor_copy(gidx[1][:], slot_row[:, 4:8]))
            for i in range(2):
                gather(i)
            pool.wait_ge(xg_turned, 1)
            take_slots(0, 0)
            own(nc.gpsimd.tensor_copy(gidx[0][:], slot_row[:, 8:12]))
            gather(0)
            before = g_steps[0]
            with pool.Fori(0, NE // 2 - 2) as c2:
                base = pool.snap(c2 * 4)
                for i in range(2):
                    work_off(i, pool.snap(c2 * 2 + i), base)
                assert g_steps[0] == before + 4
            g_steps[0] = before + 4 * (NE // 2 - 2)
            for c in range(NE - 4, NE):
                work_off(c % 2, c, 0, turned=c + 1 < NE, ahead=c + 3 < NE)
            for q, roots in ((1, ()), (2, (0,)), (3, (1, 2, 3))):
                sl = slice(ST * q, ST * (q + 1))
                pool.wait_ge(slot0_weighted, q)
                nc.gpsimd.tensor_tensor(x1_all[:, sl, :], x1_all[:, sl, :], slots[:, sl, 0:E], ALU.add
                                        ).then_inc(slot0_added, 1)
                for r in roots:
                    sl = slice(ST * r, ST * (r + 1))
                    pool.wait_ge(var_ready, 2 * ITERS + r + 1)
                    own(nc.gpsimd.tensor_scalar(var_eps[:, sl], mv[:, sl, 1], LN_EPS, None, ALU.add))
                    nc.gpsimd.tensor_tensor(rstd[:, sl], var_eps[:, sl], expo[:, sl], ALU.pow).then_inc(rstd_ready, 1)

        @block.scalar
        def _(act):
            act.dma_start(wr_sb[:], wr_t).then_inc(aux_loaded[5], 16)
            for i in range(9):
                if i < 8:
                    act.wait_ge(proj_ready, i + 1)
                    nc.scalar.copy(piece(0, i), SETUP_SLOTS[i]).then_inc(part1_ready, 1)
                if i > 0:
                    act.wait_ge(resid_ready, i)
                    nc.scalar.copy(piece(1, i - 1), resid[:, (i - 1) % 2, :]).then_inc(part2_ready, 1)
            for i in range(4):
                act.wait_ge(v_ready, i + 1)
                nc.scalar.copy(v_aug[:, 4 * i:4 * i + 4, :].rearrange("p c (h w) -> p c h w", w=VW)[:, :, :, 0:D],
                               SETUP_SLOTS[i].rearrange("p (c h d) -> p c h d", c=4, d=D)).then_inc(v_copied, 1)
            for n in range(B * NG):
                act.wait_ge(corr_ready, n + 1)
                nc.scalar.copy(corr_t[:, n, :], bank[n % 2][:, 0:2 * P]).then_inc(corr_copied, 1)
            act.wait_ge(safe_known, 1)
            with act.If(act.value_load(is_safe[:]) == 0):
                act.wait_ge(batch_stored, 2)
                for i in range(2):
                    act.wait_ge(operands_loaded[i], UNIT_DMAS * 16)
                with act.Fori(0, B) as b:
                    for g in range(NG):
                        for a in range(2):
                            rows = slice(a * HROWS, a * HROWS + KROWS)
                            for op, to in ((k_op, max_k), (q_op, max_q)):
                                act.dma_start(to[rows, :, :],
                                              op[bass.ds(b, 1), 2 * g:2 * g + 2, a].rearrange("o p r s -> r (o p) s")
                                              ).then_inc(max_loaded, 16)
                        act.wait_ge(max_split, act.snap(b * NG + g + 1))
                        for j in range(MROWS):
                            act.dma_start(q_op[bass.ds(b, 1), 2 * g:2 * g + 2, :, ROWS + j, :]
                                          .rearrange("o p a (t s) -> (o p a) t s", s=P),
                                          max_part[:, j, :]).then_inc(max_stored, 16)
                        act.wait_ge(max_stored, act.snap(b * (NG * MROWS * 16) + (g + 1) * MROWS * 16))
                    settle(act)
                for i in range(2):
                    for a in range(2):
                        act.dma_start(q_g[i][a * HROWS:a * HROWS + KROWS, :, :],
                                      q_op[0, 2 * i:2 * i + 2, a, :, 0:HALF].rearrange("p r s -> r p s")
                                      ).then_inc(max_loaded, 16)
                act.wait_ge(max_loaded, B * NG * 64 + 64)
            act.sem_inc(maxima_known, 1)
            with act.Fori(0, ITERS) as it:
                for n in range(GPI):
                    size = len(GROUPS[n % GPU])
                    act.wait_ge(scores_ready, act.snap(it * GPI + n + 1))
                    nc.scalar.activation(probs[:, n % RING, 0:size, :], scores[n % 2][:, 0:size, :], ACT.Exp,
                                         scale=SCALE).then_inc(probs_ready, 1)
            act.wait_ge(gap_ready, 1)
            nc.scalar.activation(e_gap[:], gap[:], ACT.Exp).then_inc(e_ready, 1)
            act.wait_ge(const_step, CONST_STEPS)
            nc.scalar.activation(act_spare[:], ones[:, 0:1], ACT.Gelu)
            with act.Fori(0, NE // 2) as c2:
                for i in range(2):
                    for f in range(FC):
                        act.wait_ge(hidden_ready, act.snap(c2 * (2 * FC) + i * FC + f + 1))
                        nc.scalar.activation(h_t[i][:, f, :], SETUP_SLOTS[f], ACT.Gelu).then_inc(gelu_done, 1)

            act.wait_ge(weights_ready, 1)
            for q in range(1, 4):
                act.wait_ge(slots_loaded[q], 16)
                for t in range(ST * q, ST * (q + 1)):
                    ins = nc.scalar.activation(slots[:, t, 0:E], slots[:, t, 0:E], ACT.Identity,
                                               scale=w_pair[:, 0, t:t + 1])
                ins.then_inc(slot0_weighted, 1)
            for q in range(4):
                act.wait_ge(shift_ready, q + 1)
                for t in range(ST * q, ST * (q + 1) if q < 3 else NT - ST // 2):
                    ins = nc.scalar.activation(x1_all[:, t, :], x1_all[:, t, :], ACT.Identity,
                                               bias=shift[:, t:t + 1], scale=rstd[:, t:t + 1])
                ins.then_inc(out_ready, 1)

        @block.tensor
        def _(pe):
            pe.sem_inc(unit_done, 2)
            pe.sem_inc(chunk_done, 2)
            pe.wait_ge(wx_loaded[4], 16)

            def keep_clock_up(n):
                for _ in range(n):
                    nc.tensor.matmul(bank[1][:], ones_bf[:], part[0][:, 0, 0:HALF], start=True, stop=True)

            for i in range(8):
                b, t, th = i // 4, i % 2, i // 2 % 2
                if t == 0:
                    pe.wait_ge(wx_loaded[2 * b + th], 16)
                tok = b * S + th * HALF
                nc.tensor.matmul(SETUP_SLOTS[i], wqkv_sb[:, t * E:(t + 1) * E], xt_sb[:, tok:tok + HALF],
                                 start=True, stop=True).then_inc(proj_ready, 1)
            for i in range(4):
                pe.wait_ge(resid_ready, i + 1)
                for c in range(4):
                    tok = (4 * i + c) * P
                    last = nc.tensor.matmul(SETUP_SLOTS[i][:, c * E:(c + 1) * E], xt_sb[:, tok:tok + P],
                                            wqkv_sb[:, 2 * E:3 * E], start=True, stop=True)
                last.then_inc(v_ready, 1)
            pe.wait_ge(const_step, CONST_STEPS)
            pe.wait_ge(aux_loaded[0], 16)
            pe.wait_ge(aux_loaded[5], 16)
            for b in range(B):
                for g in range(NG):
                    n = b * NG + g
                    if n == 0:
                        pe.wait_ge(resid_ready, 8)
                    if g == 0:
                        pe.wait_ge(v_copied, 2 * (b + 1))
                    if n == NG:
                        pe.wait_ge(bound_ready, 1)
                        nc.tensor.matmul(SETUP_SLOTS[4][0:1, 0:P], bound[:], ident[:], start=True, stop=True
                                         ).then_inc(bound_turned, 1)
                    if n >= 2:
                        pe.wait_ge(corr_copied, n - 1)
                    for kc, cols in ((KC - 1, slice(0, 2 * P)), (KC - 2, slice(P, 2 * P))):
                        for hh in range(GH):
                            h = GH * g + hh
                            last = nc.tensor.matmul(bank[n % 2][32 * hh:32 * hh + VW, 0:cols.stop - cols.start],
                                                    v_aug[:, b * KC + kc, h * VW:(h + 1) * VW], toep[:, h, cols],
                                                    start=(kc == KC - 1), stop=(kc == KC - 2))
                    last.then_inc(corr_ready, 1)
            for bb in range(B):
                pe.wait_ge(vsum_ready, bb + 1)
                last = nc.tensor.matmul(SETUP_SLOTS[2 + 3 * bb][:, 0:3 * E], ones[:],
                                        vsum[:, bb].rearrange("p k e -> p (k e)"), start=True, stop=True)
            last = nc.tensor.matmul(SETUP_SLOTS[5][:, 3 * E:3 * E + NE], ones[:], wr_sb[:],
                                    start=True, stop=True)
            last.then_inc(base_ready, 1)
            for b in range(B):
                pe.wait_ge(corr_copied, NG * (b + 1))
                if b == 1:
                    pe.wait_ge(safe_known, 1)
                for g in range(NG):
                    for st in range(2):
                        last = nc.tensor.transpose(scores[b][:, st, g * P:(g + 1) * P],
                                                   corr_t[:, b * NG + g, st * P:(st + 1) * P], ident[:])
                last.then_inc(corr_turned, 1)
            keep_clock_up(8)
            pe.wait_ge(bias_ready, 2)
            pe.wait_ge(wr_centred, 1)

            def score_group(n, i, k, u):
                if k == 0:
                    pe.wait_ge(operands_loaded[i], u)
                for j, (c, hh) in enumerate(GROUPS[k]):
                    pair, a = hh // 2, hh % 2
                    rows = slice(a * HROWS, (a + 1) * HROWS)
                    last = nc.tensor.matmul(scores[n % 2][:, j, :], k_g[i][rows, pair, c * P:(c + 1) * P],
                                            q_g[i][rows, pair, :], start=True, stop=True)
                last.then_inc(scores_ready, 1)

            def value_group(n, i, k):
                for j, (c, hh) in enumerate(GROUPS[k]):
                    last = nc.tensor.matmul(bank[i][32 * hh:32 * hh + VW, :], v_g[i][:, c, hh * VW:(hh + 1) * VW],
                                            probs[:, n % RING, j, :], start=(c == 0), stop=(c == KC - 1))
                if k == GPU - 1:
                    last.then_inc(unit_done, 1)

            def turn_outputs(u, it, wait):
                i = u % 2
                pe.wait_ge(out_copied, wait)
                for st in range(ST):
                    last = nc.tensor.transpose(bank[i][:, st * P:(st + 1) * P], out_t[i][:, st * P:(st + 1) * P],
                                               ident[:])
                last.then_inc(out_turned, 1)

            def turn_y(it, units_read):
                pe.wait_ge(y_ln_ready, it + 1)
                pe.wait_ge(out_read, units_read + 1)
                for t in range(ST):
                    last = nc.tensor.transpose(bank[0][:, t * P:(t + 1) * P], y_ln[:, t, :], ident[:])
                last.then_inc(y_ln_turned, 1)

            def route_logits(it):
                pe.wait_ge(y_ln_t_copied, it + 1)
                for t in range(ST):
                    last = nc.tensor.matmul(bank[0][:, t * NE:(t + 1) * NE], y_ln_t[:, t * P:(t + 1) * P], wr_c[:],
                                            start=True, stop=True)
                last.then_inc(logits_ready, 1)

            def route_ranks(it):
                pe.wait_ge(mask_ready, it + 1)
                for t in range(ST):
                    o = bank[0][:, t * NE:(t + 1) * NE]
                    nc.tensor.matmul(o, ones_bf[:], carry_bf[:], start=True, stop=False)
                    for s in range(t):
                        nc.tensor.matmul(o, ones_bf[:], mask[:, s, :], start=False, stop=False)
                    last = nc.tensor.matmul(o, tri[:], mask[:, t, :], start=False, stop=True)
                last.then_inc(ranks_ready, 1)

            def unit(u, it, hooks=(), ahead=True):
                i = u % 2
                hooks = dict(hooks)
                for k in range(GPU):
                    n = u * GPU + k
                    pe.wait_ge(probs_ready, it * GPI + n + 1)
                    if k + 2 < GPU:
                        score_group(n + 2, i, k + 2, None)
                    elif ahead:
                        nu = u + 1
                        score_group(n + 2, nu % 2, k + 2 - GPU,
                                    it * (UNIT_DMAS * 16 * 2) + UNIT_DMAS * 16 * (nu // 2 + 1))
                    if k == 0 and not (isinstance(it, int) and it == 0 and u == 0):
                        pe.wait_ge(out_read, it * ITER_UNITS + u)
                        if u == ROUTE_UNIT + 1:
                            pe.wait_ge(ranks_read, it + 1)
                    value_group(n, i, k)
                    if k == 2 and not (isinstance(it, int) and it == 0 and u == 0):
                        turn_outputs((u - 1) % ITER_UNITS, it, it * ITER_UNITS + u)
                    if k in hooks:
                        hooks[k]()

            with pe.If(pe.value_load(is_safe[:]) == 0):
                with pe.Fori(0, B * NG) as n:
                    pe.wait_ge(max_loaded, pe.snap(n * 64 + 64))
                    for j in range(GH * KC):
                        pair, a, st = j // KC // 2, j // KC % 2, j % KC
                        rows = slice(a * HROWS, a * HROWS + ROWS)
                        pe.wait_ge(max_taken, pe.snap(n * (GH * KC) + j + 1))
                        for c in range(2):
                            last = nc.tensor.matmul(scores[j % 2][:, c, :], max_q[rows, pair, st * P:(st + 1) * P],
                                                    max_k[rows, pair, c * HALF:(c + 1) * HALF], start=True, stop=True)
                        last.then_inc(max_scores, 1)
                    pe.wait_ge(max_taken, pe.snap(n * (GH * KC) + GH * KC + 2))
                    nc.tensor.transpose(bank[0][0:GH * KC, 0:P], row_max[:], ident[:]).then_inc(max_turned, 1)
            pe.wait_ge(operands_loaded[0], UNIT_DMAS * 16)
            pe.wait_ge(maxima_known, 1)
            for k in range(2):
                for j, (c, hh) in enumerate(GROUPS[k]):
                    pair, a = hh // 2, hh % 2
                    rows = slice(a * HROWS, (a + 1) * HROWS)
                    last = nc.tensor.matmul(scores[k][:, j, :], k_g[0][rows, pair, c * P:(c + 1) * P],
                                            q_g[0][rows, pair, :], start=True, stop=True)
                last.then_inc(scores_ready, 1)
            unit(0, 0)
            unit(1, 0)
            with pe.Fori(0, ITERS - 1) as it_reg:
                it = pe.snap(it_reg)
                unit(2, it)
                unit(3, it)
                nxt = pe.snap(it_reg + 1)
                unit(0, nxt)
                unit(1, nxt, hooks={6: lambda: turn_y(it, it * ITER_UNITS + ITER_UNITS + 1), 8: lambda: route_logits(it),
                                      10: lambda: route_ranks(it)})
            unit(2, ITERS - 1)
            unit(3, ITERS - 1, ahead=False)
            turn_outputs(3, ITERS - 1, UNITS)
            turn_y(ITERS - 1, UNITS)
            route_logits(ITERS - 1)
            route_ranks(ITERS - 1)
            pe.wait_ge(ranks_read, ITERS + 1)
            pe.wait_ge(rows_ready, ITERS)
            nc.tensor.matmul(bank[0][:, 0:NE], ones_bf[:], carry_bf[:], start=True, stop=True).then_inc(counts_ready, 1)

            def turn_rows(i, c, n):
                pe.wait_ge(gathered[i], n)
                for t in range(4):
                    last = nc.tensor.transpose(bank[i][:, t * P:(t + 1) * P], xg[i][:, t, 0:E], ident[:])
                last.then_inc(xg_turned, 1)

            def first_product(i, c, n):
                pe.wait_ge(w_loaded[i], n)
                pe.wait_ge(xg_copied, c + 1)
                for f in range(FC):
                    nc.tensor.matmul(SETUP_SLOTS[f], w1_g[i][:, f * P:(f + 1) * P], xg_t[i], start=True, stop=True
                                     ).then_inc(hidden_ready, 1)

            def second_product(i, c, n):
                pe.wait_ge(gelu_done, n)
                for f in range(FC):
                    last = nc.tensor.matmul(SETUP_SLOTS[4], w2_g[i][:, f, :], h_t[i][:, f, :],
                                            start=(f == 0), stop=(f == FC - 1))
                last.then_inc(chunk_done, 1)

            def turn_out(c):
                pe.wait_ge(y_copied, c + 1)
                for t in range(4):
                    last = nc.tensor.transpose(SETUP_SLOTS[5][:, t * P:(t + 1) * P], y_t[:, t * P:(t + 1) * P], ident[:])
                last.then_inc(y_turned, 1)

            def chunk(i, c, last=False):
                if not last:
                    n = 1 - i
                    turn_rows(n, c + 1, c * 32 + (64 + 32 * i))
                    second_product(i, c, c * FC + FC)
                    first_product(n, c + 1, c * 16 + (32 + 16 * i))
                else:
                    second_product(i, c, c * FC + FC)
                turn_out(c)

            pe.wait_ge(slots_known, 1)
            pe.wait_ge(rows_sent, ITERS * 2 * ST * 16)
            keep_clock_up(16)
            turn_rows(0, 0, 64)
            first_product(0, 0, 32)
            with pe.Fori(0, NE // 2 - 1) as c2:
                for i in range(2):
                    chunk(i, pe.snap(c2 * 2 + i))
            chunk(0, NE - 2)
            chunk(1, NE - 1, last=True)

        @block.vector
        def _(dve):
            dve.sem_inc(out_read, 1)
            dve.sem_inc(ranks_read, 1)
            steps = [0]

            def own(ins, base=0):
                steps[0] += 1
                ins.then_inc(v_step, 1)
                dve.wait_ge(v_step, base + steps[0])

            for i in range(9):
                if i < 8:
                    dve.wait_ge(part1_ready, i + 1)
                    if i >= 2:
                        dve.wait_ge(part3_ready, i - 1)
                    nc.vector.tensor_tensor(resid[:, i % 2, :], SETUP_SLOTS[i], piece(0, i), ALU.subtract
                                            ).then_inc(resid_ready, 1)
                if i > 0:
                    dve.wait_ge(part2_ready, i)
                    nc.vector.tensor_tensor(piece(2, i - 1), resid[:, (i - 1) % 2, :], piece(1, i - 1), ALU.subtract
                                            ).then_inc(part3_ready, 1)
            for t in range(2):
                ins = nc.vector.tensor_reduce(qk_max[:, t:t + 1], part[0][:, t, :], AX_X, ALU.max,
                                              apply_absolute_value=True)
            own(ins)
            nc.vector.tensor_tensor(bound[:], qk_max[:, 0:1], qk_max[:, 1:2], ALU.mult).then_inc(bound_ready, 1)
            dve.wait_ge(const_step, CONST_STEPS)
            for b in range(B):
                dve.wait_ge(v_copied, 2 * (b + 1))
                va = v_aug[:, b * KC:(b + 1) * KC, :].rearrange("p c (h w) -> p h w c", w=VW)
                vs = [vsum[:, b, k].rearrange("p (h d) -> p h d", d=D) for k in range(3)]
                own(nc.vector.tensor_reduce(vs[0], va[:, :, 0:D, 0:KC - 2], AX_X, ALU.add))
                own(nc.vector.tensor_tensor(vs[1], vs[0], va[:, :, 0:D, KC - 2], ALU.add))
                nc.vector.tensor_tensor(vs[2], vs[1], va[:, :, 0:D, KC - 1], ALU.add).then_inc(vsum_ready, 1)
            dve.wait_ge(bound_turned, 1)
            own(nc.vector.tensor_reduce(head_bound[:], SETUP_SLOTS[4][0:1, 0:P].rearrange("p (h d) -> p h d", d=D),
                                        AX_X, ALU.add))
            own(nc.vector.tensor_reduce(bound_max[:], head_bound[:], AX_X, ALU.max))
            nc.vector.tensor_scalar(is_safe[:], bound_max[:], SAFE / (SCALE * 1.01), None, ALU.is_le
                                    ).then_inc(safe_known, 1)
            dve.wait_ge(base_ready, 1)
            dve.wait_ge(aux_loaded[4], 16)
            nc.vector.scalar_tensor_tensor(out=wr_c[:], in0=SETUP_SLOTS[5][:, 3 * E:3 * E + NE], scalar=-1.0 / E,
                                           in1=wr_sb[:], op0=ALU.mult, op1=ALU.add).then_inc(wr_centred, 1)
            for b in range(B):
                own(nc.vector.tensor_tensor(ubase[:, b], SETUP_SLOTS[2 + 3 * b][:, 0:3 * E].rearrange("p (k e) -> p k e", k=3),
                                            last_bc[:].unsqueeze(1).broadcast_to([P, 3, E]), ALU.mult))
            for b in range(B):
                dve.wait_ge(corr_turned, b + 1)
                nc.vector.tensor_tensor(
                    bias_out[:, b * KC:b * KC + 2, :].rearrange("p t (h d) -> p t h d", d=D),
                    scores[b][:, 0:2, :].rearrange("p t (h w) -> p t h w", w=VW)[:, :, :, 0:D],
                    ubase[:, b, 0:2, :].rearrange("p t (h d) -> p t h d", d=D), ALU.add).then_inc(bias_ready, 1)
            for b in range(B):
                ins = nc.vector.tensor_copy(bias_out[:, b * KC + 2:(b + 1) * KC, :],
                                            ubase[:, b, 2:3, :].broadcast_to([P, KC - 2, E]))
            own(ins)

            dve.sem_inc(max_taken, 2)
            dve.wait_ge(safe_known, 1)
            with dve.If(dve.value_load(is_safe[:]) == 0):
                with dve.Fori(0, B * NG) as n:
                    for j in range(GH * KC):
                        dve.wait_ge(max_scores, dve.snap(n * (GH * KC) + j + 1))
                        nc.vector.tensor_reduce(row_max[:, j:j + 1], scores[j % 2][:, 0:2, :].rearrange("p c s -> p (c s)"),
                                                AX_X, ALU.max).then_inc(max_taken, 1)
                    dve.wait_ge(max_turned, dve.snap(n + 1))
                    nc.vector.tensor_scalar(neg_max[:, 0, :], bank[0][0:GH * KC, 0:P], -1.0, None, ALU.mult
                                            ).then_inc(max_step, 1)
                    dve.wait_ge(max_step, dve.snap(n * 4 + 1))
                    nc.vector.tensor_copy(max_part[:, 0, :], neg_max[:, 0, :]).then_inc(max_step, 1)
                    dve.wait_ge(max_step, dve.snap(n * 4 + 2))
                    nc.vector.tensor_tensor(neg_max[:, 1, :], neg_max[:, 0, :], max_part[:, 0, :], ALU.subtract
                                            ).then_inc(max_step, 1)
                    dve.wait_ge(max_step, dve.snap(n * 4 + 3))
                    nc.vector.tensor_copy(max_part[:, 1, :], neg_max[:, 1, :]).then_inc(max_step, 1)
                    dve.wait_ge(max_step, dve.snap(n * 4 + 4))
                    nc.vector.tensor_tensor(max_part[:, 2, :], neg_max[:, 1, :], max_part[:, 1, :], ALU.subtract
                                            ).then_inc(max_split, 1)

            def read_unit(u, it):
                i = u % 2
                dve.wait_ge(unit_done, it * ITER_UNITS + u + 3)
                nc.vector.tensor_copy(out_t[i][:], bank[i][:]).then_inc(out_copied, 1)
                dve.wait_ge(out_turned, it * ITER_UNITS + u + 1)
                turned = bank[i][:].rearrange("p (t h w) -> p t h w", t=ST, w=VW)
                own(nc.vector.reciprocal(rden[:], turned[:, :, :, D]), base[0])
                nc.vector.tensor_tensor(
                    attn[:, :, u * GH * D:(u + 1) * GH * D].rearrange("p t (h d) -> p t h d", d=D),
                    turned[:, :, :, 0:D], rden[:].unsqueeze(3).broadcast_to([P, ST, GH, D]), ALU.mult
                ).then_inc(out_read, 1)

            base = [0]

            def statistics(src, n, at=0):
                for t in range(n):
                    ins = nc.vector.bn_stats(stats[:, at + t, :], src(t))
                own(ins, base[0])
                settle(dve)
                for t in range(n):
                    ins = nc.vector.bn_aggr(mv[:, at + t, :], stats[:, at + t, :])
                ins.then_inc(var_ready, 1)

            def normalise(out_ap, src, n, at=0):
                for t in range(n):
                    ins = nc.vector.tensor_scalar(out_ap(t), src(t), mv[:, at + t, 0:1], rstd[:, at + t:at + t + 1],
                                                  ALU.subtract, ALU.mult)
                return ins

            def first_norm(it):
                dve.wait_ge(out_read, it * ITER_UNITS + ITER_UNITS + 1)
                own(nc.vector.tensor_tensor(attn[:], attn[:], bias_out[:, bass.ds(it * ST, ST), :], ALU.add), base[0])
                statistics(lambda t: attn[:, t, :], ST)
                dve.wait_ge(var_ready, it * 2 + 1)
                for t in range(ST):
                    ins = nc.vector.scalar_tensor_tensor(out=y_ln[:, t, :], in0=attn[:, t, :], scalar=mv[:, t, 0:1],
                                                         in1=gamma_bc[:], op0=ALU.subtract, op1=ALU.mult)
                own(ins, base[0])
                dve.wait_ge(rstd_ready, it * 2 + 1)
                for t in range(ST):
                    ins = nc.vector.scalar_tensor_tensor(out=y_ln[:, t, :], in0=y_ln[:, t, :], scalar=rstd[:, t:t + 1],
                                                         in1=xb[:, bass.ds(it * ST + t, 1), :].rearrange("p o e -> p (o e)"),
                                                         op0=ALU.mult, op1=ALU.add)
                ins.then_inc(y_ln_ready, 1)
                dve.wait_ge(y_ln_ready, it + 1)
                statistics(lambda t: y_ln[:, t, :], ST)

            def second_norm(it):
                dve.wait_ge(rstd_ready, it * 2 + 2)
                dve.wait_ge(pay_free, it + 1)
                normalise(lambda t: pay[0][:, t, 0:E], lambda t: y_ln[:, t, :], ST).then_inc(x1_ready, 1)

            def take_turned(it):
                dve.wait_ge(y_ln_turned, it + 1)
                nc.vector.tensor_copy(y_ln_t[:], bank[0][:]).then_inc(y_ln_t_copied, 1)

            def route(it):
                dve.wait_ge(logits_ready, it + 1)
                own(nc.vector.tensor_copy(logits[:], bank[0][:, 0:ST * NE].rearrange("p (t e) -> p t e", e=NE)), base[0])
                settle(dve)
                for t in range(ST):
                    ins = nc.vector.max(top8[:, t, :], logits[:, t, :])
                own(ins, base[0])
                settle(dve)
                for t in range(ST):
                    ins = nc.vector.max_index(idx8[:, t, :], top8[:, t, :], logits[:, t, :])
                own(ins, base[0])
                nc.vector.tensor_tensor(vals[:, :, bass.ds(it * ST, ST)], top8[:, :, 0:2].rearrange("p t k -> p k t"),
                                        rstd[:, 0:ST].unsqueeze(1).broadcast_to([P, 2, ST]), ALU.mult)
                own(nc.vector.tensor_copy(idx_f[:], idx8[:, :, 0:2].rearrange("p t k -> p k t")), base[0])
                for k in range(2):
                    ins = nc.vector.tensor_tensor(onehot[:, k], iota8[:],
                                                  idx_f[:, k].unsqueeze(2).broadcast_to([P, ST, NE]), ALU.is_equal)
                own(ins, base[0])
                nc.vector.tensor_tensor(mask[:], onehot[:, 0], onehot[:, 1], ALU.add).then_inc(mask_ready, 1)
                dve.wait_ge(ranks_ready, it + 1)
                ranks = bank[0][:, 0:ST * NE].rearrange("p (t e) -> p t e", e=NE)
                nc.vector.tensor_tensor(picked[:, 0], onehot[:, 0], ranks, ALU.mult)
                nc.vector.tensor_tensor(picked[:, 1], onehot[:, 1], ranks, ALU.mult).then_inc(ranks_read, 1)
                dve.wait_ge(ranks_read, it + 2)
                nc.vector.tensor_reduce(mask_sum[:], mask[:].rearrange("p t e -> p e t"), AX_X, ALU.add)
                own(nc.vector.tensor_reduce(rank[:], picked[:], AX_X, ALU.add), base[0])
                own(nc.vector.tensor_tensor(carry[:], carry[:], mask_sum[:], ALU.add), base[0])
                nc.vector.tensor_copy(carry_bf[:], carry[:])
                nc.vector.scalar_tensor_tensor(out=row_idx[:], in0=idx_f[:], scalar=float(N), in1=rank[:],
                                               op0=ALU.mult, op1=ALU.add).then_inc(rows_ready, 1)

            read_unit(0, 0)
            dve.wait_ge(aux_loaded[2], 16)
            dve.wait_ge(xb_ready, 1)
            before = steps[0]
            with dve.Fori(0, ITERS - 1) as it_reg:
                it = dve.snap(it_reg)
                base[0] = dve.snap(it_reg * V_ITER)
                read_unit(1, it)
                read_unit(2, it)
                read_unit(3, it)
                first_norm(it)
                second_norm(it)
                read_unit(0, dve.snap(it_reg + 1))
                take_turned(it)
                route(it)
                assert steps[0] - before == V_ITER, steps[0] - before
            steps[0] = before + V_ITER * (ITERS - 1)
            base[0] = 0
            for u in range(1, 4):
                read_unit(u, ITERS - 1)
            first_norm(ITERS - 1)
            take_turned(ITERS - 1)
            second_norm(ITERS - 1)
            route(ITERS - 1)

            dve.wait_ge(counts_ready, 1)
            own(nc.vector.tensor_copy(counts[:], bank[0][:, 0:NE]))
            own(nc.vector.tensor_tensor_scan(ends[:], counts[:], iota8[:, 0, :], 0.0, ALU.add, ALU.bypass))
            own(nc.vector.tensor_scalar(skips[:], counts[:], -1.0, float(N), ALU.mult, ALU.add))
            for e in range(NE - 1):
                ins = nc.vector.tensor_scalar(slot_add[:, e, :], slot_j[:], ends[:, e:e + 1], skips[:, e:e + 1],
                                              ALU.is_ge, ALU.mult)
            own(ins)
            own(nc.vector.tensor_reduce(slot_f[:], slot_add[:].rearrange("p e j -> p j e"), AX_X, ALU.add))
            nc.vector.tensor_tensor(slot_row[:], slot_f[:], slot_j[:], ALU.add).then_inc(slots_known, 1)
            nc.vector.tensor_tensor(gap[:], vals[:, 1], vals[:, 0], ALU.subtract).then_inc(gap_ready, 1)
            dve.wait_ge(e_ready, 1)
            own(nc.vector.tensor_scalar(gap[:], e_gap[:], 1.0, None, ALU.add))
            own(nc.vector.reciprocal(w_pair[:, 0], gap[:]))
            own(nc.vector.tensor_tensor(w_pair[:, 1], w_pair[:, 0], e_gap[:], ALU.mult))
            dve.sem_inc(weights_ready, 1)

            def copy_rows(i, c):
                dve.wait_ge(xg_turned, c + 1)
                nc.vector.tensor_copy(xg_t[i], bank[i][:]).then_inc(xg_copied, 1)

            def copy_y(i, c, first=False):
                dve.wait_ge(chunk_done, c + 3)
                nc.vector.tensor_copy(y_t, SETUP_SLOTS[4]).then_inc(y_copied, 1)
                dve.wait_ge(y_turned, c + 1)
                if not first:
                    dve.wait_ge(slots_sent[i], c * 32 - 32 * i)
                nc.vector.tensor_copy(y_g[i], SETUP_SLOTS[5].rearrange("p (t d) -> p t d", d=E)).then_inc(y_ready, 1)

            copy_rows(0, 0)
            for c in range(2):
                copy_rows(1 - c, c + 1)
                copy_y(c, c, first=True)
            with dve.Fori(1, NE // 2 - 1) as c2:
                for i in range(2):
                    c = dve.snap(c2 * 2 + i)
                    copy_rows(1 - i, dve.snap(c2 * 2 + i + 1))
                    copy_y(i, c)
            copy_rows(1, NE - 1)
            copy_y(0, NE - 2)
            copy_y(1, NE - 1)

            for q in range(5):
                if q < 4:
                    if q == 0:
                        dve.wait_ge(slots_loaded[0], 16)
                    else:
                        dve.wait_ge(slot0_added, q)
                    for k in range(0 if q == 0 else 1, 2):
                        for t in range(ST * q, ST * (q + 1)):
                            ins = nc.vector.scalar_tensor_tensor(out=x1_all[:, t, :], in0=slots[:, t, k * E:(k + 1) * E],
                                                                 scalar=w_pair[:, k, t:t + 1], in1=x1_all[:, t, :],
                                                                 op0=ALU.mult, op1=ALU.add)
                        own(ins)
                    statistics(lambda t: x1_all[:, ST * q + t, :], ST, ST * q)
                if q > 0:
                    sl = slice(ST * (q - 1), ST * q)
                    dve.wait_ge(rstd_ready, 2 * ITERS + q)
                    nc.vector.scalar_tensor_tensor(out=shift[:, sl], in0=mv[:, sl, 0], scalar=-1.0, in1=rstd[:, sl],
                                                   op0=ALU.mult, op1=ALU.mult).then_inc(shift_ready, 1)
            at = NT - ST // 2
            normalise(lambda t: x1_all[:, at + t, :], lambda t: x1_all[:, at + t, :], ST // 2, at
                      ).then_inc(last_ready, 1)


_SHAPES = [("out_0_dram", (N, E))]


def kernel(**inputs):
    import concourse.bacc as bacc
    from concourse.bass_utils import run_bass_kernel_spmd as run

    nc = bacc.Bacc("TRN2", target_bir_lowering=False, num_devices=1)
    x = np.asarray(inputs["L0_attn_x"]).reshape(N, E)
    table = np.asarray(inputs["L0_attn_bias_table"])
    rows = np.minimum(P - 1 + np.arange(2 * P)[None, :] - np.arange(P)[:, None], TABLE - 1)
    arrays = {
        "x_rows": x,
        "x_t": x.T,
        "w_qkv_t": np.concatenate([np.asarray(inputs[f"L0_attn_W{w}"]).T for w in "qkv"], axis=1),
        "bias_toeplitz": table[rows].transpose(0, 2, 1),
        "bias_last": np.repeat(table[TABLE - 1], D)[None, :],
        "gamma": np.asarray(inputs["L0_attn_ln_gamma"])[None, :],
        "beta": np.asarray(inputs["L0_attn_ln_beta"])[None, :],
        "wr_t": np.asarray(inputs["L0_ffn_Wr"]).T,
        "w1": np.asarray(inputs["L0_ffn_W1"]),
        "w2": np.asarray(inputs["L0_ffn_W2"]),
    }
    arrays = {f"in_{n}": np.ascontiguousarray(a) for n, a in arrays.items()}
    args = [nc.dram_tensor(n, a.shape, mybir.dt.from_np(a.dtype), kind="ExternalInput").ap() for n, a in arrays.items()]
    out = nc.dram_tensor("out_y", (N, E), F32, kind="ExternalOutput").ap()
    build(nc, *args, out)
    r = run(nc, [arrays], core_ids=[0])
    return r.results[0]["out_y"].reshape(B, S, E)
```
